# Optimizing a Trainium2 kernel written in Bass

```python
import numpy as np
import jax
import jax.numpy as jnp

def _softmax(x, axis=-1):
    return jax.nn.softmax(x, axis=axis)

def _gelu(x):
    return jax.nn.gelu(x, approximate=True)

def _silu(x):
    return jax.nn.silu(x)

def _sigmoid(x):
    return jax.nn.sigmoid(x)

def _layernorm(x, axis=-1, eps=1e-05):
    m = jnp.mean(x, axis=axis, keepdims=True)
    v = jnp.var(x, axis=axis, keepdims=True)
    return (x - m) / jnp.sqrt(v + eps)

def _scatter_add(tgt, idx, src, axis=0):
    return tgt.at[idx].add(src)

def _segment_sum(src, seg, n):
    return jax.ops.segment_sum(src, seg, n)
kernel_name = 'mk_seq_preln_d2_jaxref_r8_dfd815'

def setup_inputs(seed: int=0):
    np.random.seed(seed)
    _w = jnp.asarray

    def _L0_attn_setup():
        import jax, jax.numpy as jnp
        import numpy as np
        import math
        HID_DIM = 128
        NUM_HEADS = 8
        QK_DIM = HID_DIM // 8
        key = jax.random.key(seed)
        ks = jax.random.split(key, 7)
        B, M, C = (4, 256, HID_DIM)
        gain = math.sqrt(2.0)

        def xavier(k, fan_in, fan_out):
            std = gain * math.sqrt(2.0 / (fan_in + fan_out))
            a = math.sqrt(3.0) * std
            return jax.random.uniform(k, (fan_out, fan_in), jnp.float32, -a, a)
        x = jax.random.normal(ks[0], (B, M, C), jnp.float32)
        Wq = xavier(ks[1], C, QK_DIM)
        Wk = xavier(ks[2], C, QK_DIM)
        Wv = xavier(ks[3], C, C)
        bq = jnp.zeros((QK_DIM,), jnp.float32)
        bk = jnp.zeros((QK_DIM,), jnp.float32)
        bv = jnp.zeros((C,), jnp.float32)
        gamma = jnp.zeros((1,), jnp.float32)
        return {'x': x, 'Wq': Wq, 'bq': bq, 'Wk': Wk, 'bk': bk, 'Wv': Wv, 'bv': bv, 'gamma': gamma}
    _L0_attn_in = _L0_attn_setup()

    def _L0_ffn_setup():
        import jax, jax.numpy as jnp
        import numpy as np
        E, D, H, K, SH = (64, 128, 96, 6, 192)
        ROUTED_SCALE = 2.5
        key = jax.random.key(seed)
        ks = jax.random.split(key, 9)
        s = 0.02
        return {'hidden_states': jax.random.normal(ks[0], (1, 512, D), jnp.float32), 'gate_w': jax.random.normal(ks[1], (D, E), jnp.float32) * s, 'gate_bias': jax.random.normal(ks[2], (E,), jnp.float32) * s, 'all_gate_proj': jax.random.normal(ks[3], (E, D, H), jnp.float32) * s, 'all_up_proj': jax.random.normal(ks[4], (E, D, H), jnp.float32) * s, 'all_down_proj': jax.random.normal(ks[5], (E, H, D), jnp.float32) * s, 'sh_gate': jax.random.normal(ks[6], (D, SH), jnp.float32) * s, 'sh_up': jax.random.normal(ks[7], (D, SH), jnp.float32) * s, 'sh_down': jax.random.normal(ks[8], (SH, D), jnp.float32) * s}
    _L0_ffn_in = _L0_ffn_setup()

    def _L1_attn_setup():
        import jax, jax.numpy as jnp
        import numpy as np
        EMBED_DIM = 128
        NUM_HEADS = 8
        NUM_POINTS = 4
        B, N = (4, 1024)
        key = jax.random.key(seed)
        ks = jax.random.split(key, 8)
        C, H, P = (EMBED_DIM, NUM_HEADS, NUM_POINTS)
        sc = 1.0 / np.sqrt(C)
        x = jax.random.normal(ks[0], (B, N, C), dtype=jnp.float32)
        W_off = jax.random.normal(ks[1], (C, H * P * 2), dtype=jnp.float32) * sc
        b_off = jax.random.normal(ks[2], (H * P * 2,), dtype=jnp.float32) * 0.1
        W_attn = jax.random.normal(ks[3], (C, H * P), dtype=jnp.float32) * sc
        b_attn = jax.random.normal(ks[4], (H * P,), dtype=jnp.float32) * 0.1
        W_out = jax.random.normal(ks[5], (C, C), dtype=jnp.float32) * sc
        b_out = jax.random.normal(ks[6], (C,), dtype=jnp.float32) * 0.1
        return {'x': x, 'W_off': W_off, 'b_off': b_off, 'W_attn': W_attn, 'b_attn': b_attn, 'W_out': W_out, 'b_out': b_out}
    _L1_attn_in = _L1_attn_setup()

    def _L1_ffn_setup():
        import jax, jax.numpy as jnp
        import numpy as np
        TOP_K = 2
        key = jax.random.key(seed)
        k1, k2, k3, k4 = jax.random.split(key, 4)
        B, S, H, I, E = (2, 256, 128, 512, 8)
        return {'hidden_states': jax.random.normal(k1, (B, S, H), jnp.float32), 'gate_w': jax.random.normal(k2, (E, H), jnp.float32) * 0.02, 'gate_up_proj': jax.random.normal(k3, (E, 2 * I, H), jnp.float32) * 0.02, 'down_proj': jax.random.normal(k4, (E, H, I), jnp.float32) * 0.02}
    _L1_ffn_in = _L1_ffn_setup()
    _d = {'L0_attn_x': _L0_attn_in['x'], 'L0_attn_Wq': _L0_attn_in['Wq'], 'L0_attn_bq': _L0_attn_in['bq'], 'L0_attn_Wk': _L0_attn_in['Wk'], 'L0_attn_bk': _L0_attn_in['bk'], 'L0_attn_Wv': _L0_attn_in['Wv'], 'L0_attn_bv': _L0_attn_in['bv'], 'L0_attn_gamma': _L0_attn_in['gamma'], 'L0_ffn_gate_w': _L0_ffn_in['gate_w'], 'L0_ffn_gate_bias': _L0_ffn_in['gate_bias'], 'L0_ffn_all_gate_proj': _L0_ffn_in['all_gate_proj'], 'L0_ffn_all_up_proj': _L0_ffn_in['all_up_proj'], 'L0_ffn_all_down_proj': _L0_ffn_in['all_down_proj'], 'L0_ffn_sh_gate': _L0_ffn_in['sh_gate'], 'L0_ffn_sh_up': _L0_ffn_in['sh_up'], 'L0_ffn_sh_down': _L0_ffn_in['sh_down'], 'L1_attn_W_off': _L1_attn_in['W_off'], 'L1_attn_b_off': _L1_attn_in['b_off'], 'L1_attn_W_attn': _L1_attn_in['W_attn'], 'L1_attn_b_attn': _L1_attn_in['b_attn'], 'L1_attn_W_out': _L1_attn_in['W_out'], 'L1_attn_b_out': _L1_attn_in['b_out'], 'L1_ffn_gate_w': _L1_ffn_in['gate_w'], 'L1_ffn_gate_up_proj': _L1_ffn_in['gate_up_proj'], 'L1_ffn_down_proj': _L1_ffn_in['down_proj']}
    _x0 = _d['L0_attn_x']
    _d['L0_attn_x'] = jax.random.normal(jax.random.fold_in(jax.random.key(seed), 1), (1, 2048, 128), dtype=_x0.dtype)
    del _x0
    return _d

def reference(L0_attn_x, L0_attn_Wq, L0_attn_bq, L0_attn_Wk, L0_attn_bk, L0_attn_Wv, L0_attn_bv, L0_attn_gamma, L0_ffn_gate_w, L0_ffn_gate_bias, L0_ffn_all_gate_proj, L0_ffn_all_up_proj, L0_ffn_all_down_proj, L0_ffn_sh_gate, L0_ffn_sh_up, L0_ffn_sh_down, L1_attn_W_off, L1_attn_b_off, L1_attn_W_attn, L1_attn_b_attn, L1_attn_W_out, L1_attn_b_out, L1_ffn_gate_w, L1_ffn_gate_up_proj, L1_ffn_down_proj):

    def _L0_attn_ref(x, Wq, bq, Wk, bk, Wv, bv, gamma):
        import jax, jax.numpy as jnp
        import numpy as np
        import math
        HID_DIM = 128
        NUM_HEADS = 8
        QK_DIM = HID_DIM // 8
        B, M, C = x.shape
        H = NUM_HEADS
        dqk = QK_DIM // H
        dv = C // H
        q = (x @ Wq.T + bq).reshape(B, M, H, dqk)
        k = (x @ Wk.T + bk).reshape(B, M, H, dqk)
        v = (x @ Wv.T + bv).reshape(B, M, H, dv)
        scores = jnp.einsum('bmhd,bnhd->bhmn', q, k) / math.sqrt(dqk)
        scores = jnp.where(scores >= 0, scores, 0.2 * scores)
        beta = jax.nn.softmax(scores, axis=-1)
        out = jnp.einsum('bhmn,bnhd->bmhd', beta, v).reshape(B, M, C)
        return gamma * out + x

    def _L0_ffn_ref(hidden_states, gate_w, gate_bias, all_gate_proj, all_up_proj, all_down_proj, sh_gate, sh_up, sh_down):
        import jax, jax.numpy as jnp
        import numpy as np
        E, D, H, K, SH = (64, 128, 96, 6, 192)
        ROUTED_SCALE = 2.5
        orig_shape = hidden_states.shape
        x = hidden_states.reshape(-1, orig_shape[-1])
        T = x.shape[0]
        scores = jax.nn.sigmoid(x @ gate_w)
        _, topk_idx = jax.lax.top_k(scores + gate_bias[None, :], K)
        topk_w = jnp.take_along_axis(scores, topk_idx, axis=1)
        topk_w = topk_w / (topk_w.sum(-1, keepdims=True) + 1e-20) * ROUTED_SCALE
        mask = jnp.zeros((T, E), x.dtype).at[jnp.arange(T)[:, None], topk_idx].set(topk_w)

        def body(acc, expert):
            g, u, d, m = expert
            h = jax.nn.silu(x @ g) * (x @ u)
            return (acc + h @ d * m[:, None], None)
        routed, _ = jax.lax.scan(body, jnp.zeros_like(x), (all_gate_proj, all_up_proj, all_down_proj, mask.T))
        shared = jax.nn.silu(x @ sh_gate) * (x @ sh_up) @ sh_down
        return (routed + shared).reshape(orig_shape)

    def _L1_attn_ref(x, W_off, b_off, W_attn, b_attn, W_out, b_out):
        import jax, jax.numpy as jnp
        import numpy as np
        EMBED_DIM = 128
        NUM_HEADS = 8
        NUM_POINTS = 4
        B, N = (4, 1024)
        Bx, Nx, C = x.shape
        H, P = (NUM_HEADS, NUM_POINTS)
        off = (x @ W_off + b_off).reshape(Bx, Nx, H, P, 2)
        w = jax.nn.softmax((x @ W_attn + b_attn).reshape(Bx, Nx, H, P), axis=-1)
        idx = off[..., 0].astype(jnp.int32)
        idx = jnp.where(idx < 0, idx + C, idx)
        idx = jnp.clip(idx, 0, C - 1)
        x0 = x[:, 0, :]
        g = jnp.take_along_axis(x0, idx.reshape(Bx, -1), axis=1).reshape(Bx, Nx, H, P)
        s = jnp.sum(g * w, axis=(2, 3))
        out = jnp.broadcast_to(s[..., None], (Bx, Nx, C))
        return out @ W_out + b_out

    def _L1_ffn_ref(hidden_states, gate_w, gate_up_proj, down_proj):
        import jax, jax.numpy as jnp
        import numpy as np
        TOP_K = 2
        B, S, H = hidden_states.shape
        E = gate_w.shape[0]
        x = hidden_states.reshape(-1, H)
        T = x.shape[0]
        probs = jax.nn.softmax(x @ gate_w.T, axis=-1)
        w, idx = jax.lax.top_k(probs, TOP_K)
        w = w / jnp.sum(w, axis=-1, keepdims=True)
        combine = jnp.zeros((T, E), x.dtype).at[jnp.arange(T)[:, None], idx].add(w)

        def step(acc, inputs):
            gup, dn, ce = inputs
            g, u = jnp.split(x @ gup.T, 2, axis=-1)
            acc = acc + ce[:, None] * (jax.nn.silu(g) * u @ dn.T)
            return (acc, None)
        out, _ = jax.lax.scan(step, jnp.zeros_like(x), (gate_up_proj, down_proj, combine.T))
        return out.reshape(B, S, H)
    x = L0_attn_x
    x = x + _L0_attn_ref(_layernorm(x, axis=-1), L0_attn_Wq, L0_attn_bq, L0_attn_Wk, L0_attn_bk, L0_attn_Wv, L0_attn_bv, L0_attn_gamma)
    x = x + _L0_ffn_ref(_layernorm(x, axis=-1), L0_ffn_gate_w, L0_ffn_gate_bias, L0_ffn_all_gate_proj, L0_ffn_all_up_proj, L0_ffn_all_down_proj, L0_ffn_sh_gate, L0_ffn_sh_up, L0_ffn_sh_down)
    x = x + _L1_attn_ref(_layernorm(x, axis=-1), L1_attn_W_off, L1_attn_b_off, L1_attn_W_attn, L1_attn_b_attn, L1_attn_W_out, L1_attn_b_out)
    x = x + _L1_ffn_ref(_layernorm(x, axis=-1), L1_ffn_gate_w, L1_ffn_gate_up_proj, L1_ffn_down_proj)
    return x

_drawn_inputs = setup_inputs


def setup_inputs(seed=0):
    import zlib

    import numpy as np

    out = dict(_drawn_inputs(seed))
    spreads = {'L0_attn_bq': (0.0, 0.1), 'L0_attn_bk': (0.0, 0.1), 'L0_attn_bv': (0.0, 0.1)}
    factors = {'L0_ffn_gate_w': 8.0,
     'L0_ffn_gate_bias': 8.0,
     'L0_ffn_all_gate_proj': 8.0,
     'L0_ffn_all_up_proj': 8.0,
     'L0_ffn_all_down_proj': 8.0,
     'L0_ffn_sh_gate': 6.797,
     'L0_ffn_sh_up': 6.567,
     'L0_ffn_sh_down': 7.644,
     'L1_attn_b_attn': 6.478,
     'L1_attn_b_out': 7.775,
     'L1_ffn_gate_w': 8.0,
     'L1_ffn_gate_up_proj': 8.0,
     'L1_ffn_down_proj': 8.0}
    for name, (base, spread) in spreads.items():
        noise = np.random.default_rng([zlib.crc32(name.encode()), seed]).standard_normal(out[name].shape)
        drawn = base * np.exp(spread * noise) if base else spread * noise
        out[name] = jnp.asarray(drawn.astype(out[name].dtype))
    for name, factor in factors.items():
        out[name] = (out[name] * factor).astype(out[name].dtype)
    return out
```

```python
import math
from contextlib import ExitStack

import concourse.bass as bass
import numpy as np
from concourse import mybir

P = 128
T = 2048
NT = T // P
BANK = 512
CH = 512
NC = T // CH
H = 8
DQK, DV = 2, 16
G = 2
HG = H // G
KROWS = 9 * DQK
KSC = KROWS + 3
EPS = 1e-5
E0, TOP0, SCALE0 = 64, 6, 2.5
E1, TOP1 = 8, 2
HP, PT = 32, 4
SUB0 = 3
SUB1 = 4
HALVES0 = E0 * 96 // P // SUB0
HALVES1 = E1
SEGMENTS0 = [(s, p0, p1, e) for s in range(SUB0) for e in range(4)
             for p0, p1 in [(max(96 * e - 128 * s, 0), min(96 * (e + 1) - 128 * s, 128))] if p0 < p1]

F32_COLS = [("ident", P), ("ksel", 2), ("qsel", 2), ("bval", 1), ("aval", 1), ("selx", P), ("amask", 8),
            ("bdmask", 64), ("vx", P), ("vy", P), ("ones", P), ("selw", 2 * P)]
BF_COLS = [("identb", P), ("ud", P), ("selb", 4 * P), ("sela", 2 * P)]


def columns(cols):
    at, out = 0, {}
    for name, n in cols:
        out[name] = (at, at + n)
        at += n
    return out, at


FC, NF = columns(F32_COLS)
BC, NB = columns(BF_COLS)


def constants():
    c = {}
    p = np.arange(P)
    c["ident"] = c["identb"] = np.eye(P)
    row = p % 32
    k_part = np.where(row < KROWS, row % 3, 0)
    q_part = np.where(row < KROWS, row % 9 // 3, 0)
    c["ksel"] = -np.stack([k_part >= 1, k_part >= 2], 1).astype(float)
    c["qsel"] = -np.stack([q_part >= 1, q_part >= 2], 1).astype(float)
    c["bval"] = (p % 16)[:, None]
    c["aval"] = (p % 8)[:, None]
    c["selx"] = p[:, None] % 16 == p[None, :] % 16
    c["amask"] = p[:, None] // 16 == np.arange(8)[None, :]
    c["bdmask"] = np.repeat(p[:, None] // 16 == np.arange(8)[None, :], 8, axis=1)
    angle = 2 * np.pi * p / P
    u = np.stack([np.cos(angle), np.sin(angle)], 1).astype(np.float32)
    u = ((u.view(np.uint32) + 0x8000) & 0xFFFF0000).astype(np.uint32).view(np.float32).astype(np.float64)
    ud = np.zeros((P, P))
    for h in range(HG):
        for d in range(DQK):
            for j in range(3):
                ud[32 * h + 9 * d + j] = u[:, d]
    c["ud"] = ud
    nxt = (p + 1) % P
    inv = np.linalg.inv(np.stack([u, u[nxt]], 1))
    for name, d in (("vx", 0), ("vy", 1)):
        m = np.zeros((P, P))
        m[p, p] = inv[:, d, 0]
        m[nxt, p] = inv[:, d, 1]
        c[name] = m
    c["ones"] = np.ones((P, P))
    selw, sela, selb = np.zeros((P, 2, P)), np.zeros((P, 2, P)), np.zeros((P, 4, P))
    for m in range(2):
        selw[64 + 16 * m + p // 8, m, p] = 1
        sela[32 + 16 * m + p // 8, m, p] = 1
    for k in range(4):
        selb[8 * k + p // 16, k, p] = 1
    c["selw"], c["sela"], c["selb"] = selw.reshape(P, -1), sela.reshape(P, -1), selb.reshape(P, -1)
    return np.concatenate([np.asarray(c[n], np.float32) for n, _ in F32_COLS + BF_COLS], 1)


def build(nc, a, out):
    f32, bf16 = mybir.dt.float32, mybir.dt.bfloat16
    ALU, ACT, AX = mybir.AluOpType, mybir.ActivationFunctionType, mybir.AxisListType
    ds = bass.ds

    mask0_dram = nc.dram_tensor("mask0_scratch", (E0, T), f32, kind="Internal").ap()
    mask1_dram = nc.dram_tensor("mask1_scratch", (E1, T), f32, kind="Internal").ap()

    ctx = ExitStack()
    with ctx:
        def sb(name, shape, dt=f32, stack=ctx):
            return stack.enter_context(nc.sbuf_tensor(name, shape, dt))

        sems = {}

        def sem(name):
            if name not in sems:
                sems[name] = ctx.enter_context(nc.semaphore(name))
            return sems[name]

        CF = sb("CF", [P, NF])
        CB = sb("CB", [P, NB], bf16)
        X = sb("X", [P, NT, P])
        XN = sb("XN", [P, NT, P])
        XS = sb("XS", [P, NT, P])
        XT = sb("XT", [P, T])
        YT = sb("YT", [P, T])
        WR = sb("WR", [P, 2 * SUB1, 3 * P])
        stats = sb("stats", [P, NT, 6])
        moments = sb("moments", [P, NT, 2])
        rstd = sb("rstd", [P, NT])
        half = sb("half", [P, NT])
        wvt = sb("wvt", [P, P])
        bvb = sb("bvb", [P, P])
        wqk = sb("wqk", [P, 4, P])
        bqk = sb("bqk", [P, 4])
        gam = sb("gam", [P, 1])
        gw0 = sb("gw0", [P, E0])
        gb0 = sb("gb0", [P, E0])
        wol = sb("wol", [P, 2 * HP])
        bol = sb("bol", [P, 2 * HP])
        wout = sb("wout", [P, P])
        boutb = sb("boutb", [P, P])
        gw1 = sb("gw1", [P, E1])
        small = sb("small", [P, 8, NT * H])
        PS = ctx.enter_context(nc.psum_tensor("PS", [P, 8 * BANK], f32))

        def cf(name, lo=0, hi=None):
            s, e = FC[name]
            return CF[:, s + lo:(s + hi if hi else e)]

        def cb(name, lo=0, hi=None):
            s, e = BC[name]
            return CB[:, s + lo:(s + hi if hi else e)]

        def bank(b, n=1):
            return PS[:, b * BANK:(b + n) * BANK]

        att = ExitStack()
        KS = [sb(f"KS{g}", [P, T], bf16, att) for g in range(G)]
        QA = [sb(f"QA{g}", [P, T], bf16, att) for g in range(G)]
        QB = [sb(f"QB{g}", [P, T], bf16, att) for g in range(G)]
        VS = sb("VS", [P, NT, H, 32], f32, att)
        OT = [sb(f"OT{g}", [P, T], f32, att) for g in range(G)]
        pre = ExitStack()
        F = [sb(f"F{i}", [P, T], f32, pre) for i in range(6)]
        TB = [sb(f"TB{i}", [P, T], bf16, pre) for i in range(3)]
        hm = sb("hm", [P, H], f32, pre)
        hxy = sb("hxy", [P, G, 2, P], f32, pre)
        vtx = sb("vtx", [P, G * P], f32, pre)
        vtb = sb("vtb", [P, G * P], bf16, pre)
        VV = sb("VV", [P, G * P], bf16, pre)
        mparts = sb("mparts", [P, 3, NT * H], bf16, pre)
        MR = sb("MR", [P, G, NT, P], bf16, pre)
        pre.close()
        flow = ExitStack()
        ASB = [sb(f"ASB{i}", [P, 2 * CH], f32, flow) for i in range(4)]
        LB = [sb(f"LB{i}", [P, HG, CH], f32, flow) for i in range(2)]
        PB = [sb(f"PB{i}", [P, HG, CH], f32, flow) for i in range(2)]
        QSA = sb("QSA", [P, CH], bf16, flow)
        QSB = sb("QSB", [P, CH], bf16, flow)
        flow.close()
        att.close()
        moe_mem = ExitStack()
        MK = sb("MK", [P, 2, SUB0, T], f32, moe_mem)
        SL = [sb(f"SL{i}", [P, CH], f32, moe_mem) for i in range(2)]
        SU = [sb(f"SU{i}", [P, CH], f32, moe_mem) for i in range(2)]
        HB = [sb(f"HB{i}", [P, CH], f32, moe_mem) for i in range(2)]
        sc = sb("sc", [P, NT, E0], f32, moe_mem)
        bs = sb("bs", [P, NT, E0], f32, moe_mem)
        rp = sb("rp", [P, NT, E0], f32, moe_mem)
        top8 = sb("top8", [P, NT, 8], f32, moe_mem)
        rsum = sb("rsum", [P, NT], f32, moe_mem)
        MT = sb("MT", [E0, T], f32, moe_mem)
        moe_mem.close()
        lk = ExitStack()
        OL = sb("OL", [P, NT, 2 * HP], f32, lk)
        TS = sb("TS", [P, NT, 3 * HP], f32, lk)
        ix = [sb(f"ix{i}", [P, NT, HP], f32, lk) for i in range(4)]
        iint = sb("iint", [P, NT, HP], mybir.dt.int32, lk)
        lmax = sb("lmax", [P, NT, 8], f32, lk)
        TI = sb("TI", [2 * HP, T], bf16, lk)
        TW = sb("TW", [3 * HP, T], f32, lk)
        OH = [sb(f"OH{i}", [P, T], f32, lk) for i in range(2)]
        WE = sb("WE", [P, T], f32, lk)
        AW = sb("AW", [P, T], f32, lk)
        PR = [sb(f"PR{i}", [P, T], f32, lk) for i in range(2)]
        dx = sb("dx", [P, 8], f32, lk)
        BD = sb("BD", [P, 2, P], f32, lk)
        cw = sb("cw", [P, P], f32, lk)
        lk.close()

        block = ctx.enter_context(nc.Block())

        STEPS = 2 * NT
        DVE_COPIES = [s for s in range(STEPS) if s % 10 in (2, 5, 8)]
        ACT_COPIES = [s for s in range(STEPS) if s not in DVE_COPIES]
        FILLS = 2 * STEPS

        def copied(s):
            if s in DVE_COPIES:
                return "a_copied_dve", DVE_COPIES.index(s) + 1, len(DVE_COPIES)
            return "a_copied_act", ACT_COPIES.index(s) + 1, len(ACT_COPIES)

        def units(slots):
            return [(s, c) for s in slots for c in range(NC)]

        MOE = {
            0: dict(sub=SUB0, halves=HALVES0, pro=units([SUB0 * 2 - 2, SUB0 * 2 - 1])),
            1: dict(sub=SUB1, halves=HALVES1, pro=[]),
        }
        for m in MOE.values():
            m["body"] = units(range(2 * m["sub"]))
            m["n_body"] = len(m["body"])
            m["n_pro"] = len(m["pro"])

        @block.sync
        def _(sp):
            def load(dst, src, name="loaded"):
                sp.dma_start(dst, src).then_inc(sem(name), 16)

            load(X[:, :, :], a["x"].rearrange("(t p) c -> p t c", p=P), "x_loaded")
            load(CF[:, :], a["consts"][:, 0:NF], "cf_loaded")
            load(YT[:, 0:NB], a["consts"][:, NF:NF + NB], "cb_loaded")
            load(wqk[:, :, :], a["wqk"], "qkv_loaded")
            load(bqk[:, :], a["bqk"], "qkv_loaded")
            load(wvt[:, :], a["wvt"], "qkv_loaded")
            load(bvb[:, :], a["bv"].partition_broadcast(P), "qkv_loaded")
            load(gam[:, :], a["gamma"].partition_broadcast(P), "rest_loaded")
            load(gw0[:, :], a["gw0"], "rest_loaded")
            load(gb0[:, :], a["gb0"].partition_broadcast(P), "rest_loaded")
            load(wol[:, :], a["wol"], "rest_loaded")
            load(bol[:, :], a["bol"].partition_broadcast(P), "rest_loaded")
            load(wout[:, :], a["wout"], "rest_loaded")
            load(boutb[:, :], a["bout"].partition_broadcast(P), "rest_loaded")
            load(gw1[:, :], a["gw1"], "rest_loaded")

            def moe_loads(l, weights, mask_dram):
                m = MOE[l]
                sub, nb, npro = m["sub"], m["n_body"], m["n_pro"]
                down, masked = sem(f"down_done{l}"), sem(f"h_ready{l}")

                def half(it, h, w_free, m_free):
                    if w_free is not None:
                        sp.wait_ge(down, w_free)
                    k = it * 2 + h
                    sp.dma_start(WR[:, h * sub:(h + 1) * sub, :], weights[ds(k, 1)].squeeze(0)).then_inc(
                        sem(f"w_loaded{l}_{h}"), 16)
                    if m_free is not None:
                        sp.wait_ge(masked, m_free)
                    if l == 0:
                        for s, p0, p1, e in SEGMENTS0:
                            sp.dma_start(MK[p0:p1, h, s, :], mask_dram[ds(k * 4 + e, 1), :].to_broadcast([p1 - p0, T])
                                         ).then_inc(sem(f"m_loaded{l}_{h}"), 16)
                    else:
                        sp.dma_start(MK[:, h, 0, :], mask_dram[ds(k, 1), :].to_broadcast([P, T])
                                     ).then_inc(sem(f"m_loaded{l}_{h}"), 16)

                return half, nb, npro

            sp.dma_start(WR[:, 2 * SUB0 - 2:2 * SUB0, :], a["wsh"]).then_inc(sem("wsh_loaded"), 16)
            sp.wait_ge(sem("mask_t0"), 4)
            sp.dma_start(mask0_dram[:, :], MT[:, :]).then_inc(sem("mask_stored0"), 16)
            sp.wait_ge(sem("mask_stored0"), 16)
            half, nb, npro = moe_loads(0, a["w0"], mask0_dram)
            half(0, 0, None, None)
            half(0, 1, npro, None)
            with sp.Fori(1, HALVES0 // 2) as it:
                half(it, 0, npro + (it - 1) * nb + nb // 2, npro + (it - 1) * nb + nb // 2)
                half(it, 1, npro + it * nb, npro + it * nb)

            sp.wait_ge(sem("mask_t1"), 4)
            sp.dma_start(mask1_dram[:, :], MT[0:E1, :]).then_inc(sem("mask_stored1"), 16)
            sp.wait_ge(sem("mask_stored1"), 16)
            half, nb, npro = moe_loads(1, a["w1"], mask1_dram)
            half(0, 0, None, None)
            half(0, 1, None, None)
            with sp.Fori(1, HALVES1 // 2) as it:
                half(it, 0, (it - 1) * nb + nb // 2, (it - 1) * nb + nb // 2)
                half(it, 1, it * nb, it * nb)

            for q in range(NC):
                sp.wait_ge(sem("x_moe1"), q + 1)
                sp.dma_start(out[q * CH:(q + 1) * CH, :].rearrange("(t p) c -> p t c", p=P),
                             X[:, 4 * q:4 * q + 4, :]).then_inc(sem("stored"), 16)
            sp.wait_ge(sem("stored"), 16 * NC)

        @block.tensor
        def _(pe):
            mm = nc.tensor.matmul
            ident = cf("ident")

            def transpose_norm(l):
                for q in range(NC):
                    pe.wait_ge(sem("xn_ready"), NC * l + q + 1)
                    for t in range(4 * q, 4 * q + 4):
                        last = nc.tensor.transpose(PS[:, t * P:(t + 1) * P], XN[:, t, :], ident)
                    last.then_inc(sem("xt_psum"), 1)

            pe.wait_ge(sem("cf_loaded"), 16)
            transpose_norm(0)

            pe.wait_ge(sem("xt_ready"), NC)
            pe.wait_ge(sem("qkv_loaded"), 64)
            for i in range(4):
                if i >= 2:
                    pe.wait_ge(sem("f_ready"), i - 1)
                for c in range(NC):
                    last = mm(bank(4 * ((i + 1) % 2) + c), wqk[:, i, :], XT[:, c * CH:(c + 1) * CH], start=True, stop=True)
                last.then_inc(sem("proj_done"), 1)
            pe.wait_ge(sem("f_ready"), 3)
            for t in range(NT):
                last = mm(PS[:, 4 * BANK + t * P:4 * BANK + (t + 1) * P], XT[:, t * P:(t + 1) * P], wvt[:, :], start=True, stop=True)
            last.then_inc(sem("v_psum"), 1)

            pe.wait_ge(sem("cb_ready"), 1)
            for h in range(H):
                g, j = divmod(h, HG)
                if j == 0:
                    pe.wait_ge(sem("split_ready"), g + 1)
                if h == 0:
                    pe.wait_ge(sem("f_ready"), 4)
                elif h == 1:
                    pe.wait_ge(sem("v_ready"), 1)
                else:
                    pe.wait_ge(sem("extent_ready"), h - 1)
                r = slice(32 * j, 32 * j + KROWS)
                for c in range(NC):
                    last = mm(bank(4 * (h % 2) + c), cb("ud")[r, :], KS[g][r, c * CH:(c + 1) * CH], start=True, stop=True)
                last.then_inc(sem("extent_psum"), 1)
            pe.wait_ge(sem("hxy_ready"), 1)
            for g in range(G):
                mm(PS[:, g * P:(g + 1) * P], hxy[:, g, 0, :], cf("vx"), start=True, stop=False)
                last = mm(PS[:, g * P:(g + 1) * P], hxy[:, g, 1, :], cf("vy"), start=False, stop=True)
            last.then_inc(sem("corners_psum"), 1)
            pe.wait_ge(sem("corners_ready"), 1)
            pe.wait_ge(sem("split_ready"), 4)
            for tp in range(NT // 2):
                if tp >= 2:
                    pe.wait_ge(sem("bound_ready"), tp - 1)
                for tt in range(2):
                    for g in range(G):
                        for j in range(HG):
                            r = slice(32 * j, 32 * j + KROWS)
                            t = 2 * tp + tt
                            at = (4 * (tp % 2) + j) * BANK + (2 * g + tt) * P
                            last = mm(PS[:, at:at + P], QA[g][r, t * P:(t + 1) * P], VV[r, g * P:(g + 1) * P], start=True, stop=True)
                last.then_inc(sem("bound_psum"), 1)
            pe.wait_ge(sem("mr_ready"), 1)
            for g in range(G):
                for t in range(NT):
                    last = mm(PS[:, 4 * g * BANK + t * P:4 * g * BANK + (t + 1) * P], MR[:, g, t, :], cb("identb"), start=True, stop=True)
                last.then_inc(sem("mrows_psum"), 1)
            pe.wait_ge(sem("q_final"), 4)
            pe.sem_inc(sem("q_used"), 1)

            for g in range(G):
                with pe.Fori(0, NC) as c:
                    it = c + g * NC

                    def slot_free(fill):
                        prev = fill - 3
                        s = prev // 2
                        if prev % 2 == 0:
                            name, rank, per = copied(s)
                        else:
                            name, rank, per = "l_ready", s + 1, STEPS
                        return name, it * per + rank

                    def pv(n):
                        pe.wait_ge(sem("p_ready"), it * NT + n + 1)
                        for j in range(HG):
                            last = mm(PS[32 * j:32 * j + 32, 6 * BANK:7 * BANK], VS[:, n, g * HG + j, :], PB[n % 2][:, j, :],
                                      start=(n == 0), stop=(n == NT - 1))
                            if n == NT - 2 and j == 0:
                                last.then_inc(sem("q_used"), 1)
                        last.then_inc(sem("pv_done"), 1)

                    pe.wait_ge(sem("q_staged"), it + 1)
                    for n in range(NT):
                        for hp in range(2):
                            s = 2 * n + hp
                            for fill, Q in ((2 * s, QSA), (2 * s + 1, QSB)):
                                if not (fill < 3):
                                    pe.wait_ge(sem(slot_free(fill)[0]), slot_free(fill)[1])
                                elif fill == 0:
                                    pe.wait_ge(sem("sums_taken"), it + 1)
                                for k in range(2):
                                    j = 2 * hp + k
                                    r = slice(32 * j, 32 * j + KSC)
                                    last = mm(bank(2 * (fill % 3) + k), KS[g][r, n * P:(n + 1) * P], Q[r, :], start=True, stop=True)
                                last.then_inc(sem("scores_done"), 1)
                        if n >= 1:
                            pv(n - 1)
                    pv(NT - 1)

            pe.wait_ge(sem("sums_taken"), G * NC + 1)
            for t in range(NT):
                for g in range(G):
                    last = nc.tensor.transpose(PS[:, (2 * t + g) * P:(2 * t + g + 1) * P], OT[g][:, t * P:(t + 1) * P], ident)
                if t % 4 == 3:
                    last.then_inc(sem("o_psum"), 1)

            def router(l, w, n):
                pe.wait_ge(sem("xt_ready"), NC * (2 * l + 2))
                for t in range(NT):
                    last = mm(PS[:, 4 * BANK + t * n:4 * BANK + (t + 1) * n], XT[:, t * P:(t + 1) * P], w, start=True, stop=True)
                last.then_inc(sem(f"router_psum{l}"), 1)

            def masks_back(l, src, n):
                pe.wait_ge(sem(f"mask_ready{l}"), 1)
                for t in range(NT):
                    last = nc.tensor.transpose(PS[0:n, t * P:(t + 1) * P], src[:, t, 0:n], ident)
                last.then_inc(sem(f"mask_psum{l}"), 1)

            def moe(l):
                m = MOE[l]
                nb, npro = m["n_body"], m["n_pro"]
                gu, h_ready, down_done, taken = sem(f"gu_done{l}"), sem(f"h_ready{l}"), sem(f"down_done{l}"), sem(f"su_done{l}")
                for c in range(NC):
                    for t in range(4 * c, 4 * c + 4):
                        mm(PS[:, 4 * BANK + t * P:4 * BANK + (t + 1) * P], X[:, t, :], ident,
                           start=(t == 4 * c), stop=False, skip_group_check=True)

                def down(slot, c, u, buf):
                    pe.wait_ge(h_ready, u + 1)
                    mm(bank(4 + c), WR[:, slot, 2 * P:3 * P], HB[buf][:, :], start=False, stop=False,
                       skip_group_check=True).then_inc(down_done, 1)

                def run(seq, base, prev, it=None, first=False):
                    for k, (slot, c) in enumerate(seq):
                        if it is not None and c == 0 and slot % m["sub"] == 0:
                            pe.wait_ge(sem(f"w_loaded{l}_{slot // m['sub']}"), (it + 1) * 16)
                        if not (first and k < 2):
                            pe.wait_ge(taken, base + k - 1)
                        x = XT[:, c * CH:(c + 1) * CH]
                        mm(bank(2 * (k % 2)), WR[:, slot, 0:P], x, start=True, stop=True)
                        mm(bank(2 * (k % 2) + 1), WR[:, slot, P:2 * P], x, start=True, stop=True).then_inc(gu, 1)
                        if prev is not None:
                            down(*prev, base + k - 1, (k + 1) % 2)
                        prev = (slot, c)
                    return prev

                if l == 0:
                    pe.wait_ge(sem("wsh_loaded"), 16)
                    prev = run(m["pro"], 0, None, first=True)
                    with pe.Fori(0, m["halves"] // 2) as it:
                        run(m["body"], npro + it * nb, prev, it)
                else:
                    prev = run(m["body"], 0, None, 0, first=True)
                    with pe.Fori(1, m["halves"] // 2) as it:
                        run(m["body"], it * nb, prev, it)
                total = npro + nb * m["halves"] // 2
                down(*m["body"][-1], total - 1, 1)

            def moe_back(l):
                for q in range(NC):
                    pe.wait_ge(sem("yt_ready"), NC * l + q + 1)
                    for t in range(4 * q, 4 * q + 4):
                        last = nc.tensor.transpose(PS[:, t * P:(t + 1) * P], YT[:, t * P:(t + 1) * P], ident)
                    last.then_inc(sem("y_psum"), 1)

            pe.wait_ge(sem("rest_loaded"), 16 * 8)
            transpose_norm(1)
            router(0, gw0[:, :], E0)
            masks_back(0, sc, E0)
            pe.wait_ge(sem("mask_t0"), 4)
            moe(0)
            moe_back(0)
            transpose_norm(2)

            pe.wait_ge(sem("xt_ready"), NC * 3)
            for t in range(NT):
                last = mm(PS[:, 4 * BANK + t * 64:4 * BANK + (t + 1) * 64], XT[:, t * P:(t + 1) * P], wol[:, :], start=True, stop=True)
            last.then_inc(sem("ol_psum"), 1)
            pe.wait_ge(sem("dx_ready"), 1)
            mm(PS[:, 7 * BANK:7 * BANK + P], cf("ones"), wout[:, :], start=True, stop=True)
            mm(PS[:, 7 * BANK + P:7 * BANK + P + 8], cf("selx"), dx[:, :], start=True, stop=True).then_inc(sem("tables_psum"), 1)
            pe.wait_ge(sem("ts_ready"), 1)
            for t in range(NT):
                last = nc.tensor.transpose(PS[0:96, t * P:(t + 1) * P], TS[:, t, :], ident)
            last.then_inc(sem("ts_psum"), 1)

            pe.wait_ge(sem("tables_ready"), 1)
            pe.wait_ge(sem("ti_ready"), 2)
            fills = [("b", 0), ("b", 1), ("w", 0), ("a", 0), ("r", 0), ("b", 2), ("b", 3), ("w", 1), ("a", 1), ("r", 1)]
            for f, (kind, i) in enumerate(fills):
                base = 4 if f % 2 == 0 else 0
                if f >= 2:
                    k = fills[f - 2][0]
                    n = sum((x == "w") == (k == "w") for x, _ in fills[:f - 1])
                    pe.wait_ge(sem("expanded_act" if k == "w" else "expanded_dve"), n)
                if kind == "r":
                    pe.wait_ge(sem("expanded_dve"), 2 + 4 * i)
                for c in range(NC):
                    x = slice(c * CH, (c + 1) * CH)
                    if kind == "b":
                        last = mm(bank(base + c), cb("selb")[0:32, i * P:(i + 1) * P], TI[0:32, x], start=True, stop=True)
                    elif kind == "a":
                        last = mm(bank(base + c), cb("sela")[32:64, i * P:(i + 1) * P], TI[32:64, x], start=True, stop=True)
                    elif kind == "w":
                        last = mm(bank(base + c), cf("selw")[64:96, i * P:(i + 1) * P], TW[64:96, x], start=True, stop=True)
                    else:
                        mm(bank(base + c), BD[:, 0, :], OH[0][:, x], start=True, stop=False)
                        last = mm(bank(base + c), BD[:, 1, :], OH[1][:, x], start=False, stop=True)
                last.then_inc(sem("expand_psum"), 1)
            pe.wait_ge(sem("expanded_dve"), 8)
            for t in range(NT):
                o = PS[:, 4 * BANK + t * P:4 * BANK + (t + 1) * P]
                mm(o, PR[0][:, t * P:(t + 1) * P], cw[:, :], start=True, stop=False)
                last = mm(o, PR[1][:, t * P:(t + 1) * P], cw[:, :], start=False, stop=True)
                if t % 4 == 3:
                    last.then_inc(sem("lookup_psum"), 1)

            transpose_norm(3)
            router(1, gw1[:, :], E1)
            masks_back(1, sc, E1)
            pe.wait_ge(sem("mask_t1"), 4)
            moe(1)
            moe_back(1)

        @block.scalar
        def _(act):
            A = nc.scalar.activation

            def norm_out(l):
                for q in range(NC):
                    act.wait_ge(sem("xt_psum"), NC * l + q + 1)
                    nc.scalar.copy(XT[:, q * CH:(q + 1) * CH], bank(q)).then_inc(sem("xt_ready"), 1)

            norm_out(0)
            for i in range(6):
                for step in range(2):
                    if step == 0:
                        act.wait_ge(sem("f_ready") if i < 4 else sem("f_scaled"), i + 1 if i < 4 else i - 3)
                        if i >= 3:
                            act.wait_ge(sem("split_ready"), i - 2)
                    else:
                        act.wait_ge(sem("rest1_ready"), i + 1)
                    nc.scalar.copy(TB[i % 3][:, :], F[i][:, :]).then_inc(sem("part_ready"), 1)

            for g in range(G):
                with act.Fori(0, NC) as c:
                    it = c + g * NC

                    def exponential(n):
                        act.wait_ge(sem("l_ready"), it * STEPS + 2 * n + 2)
                        if n >= 2:
                            act.wait_ge(sem("pv_done"), it * NT + n - 1)
                        A(PB[n % 2][:, :, :], LB[n % 2][:, :, :], ACT.Exp).then_inc(sem("p_ready"), 1)

                    for n in range(NT):
                        for s in (2 * n, 2 * n + 1):
                            if s in ACT_COPIES:
                                act.wait_ge(sem("scores_done"), it * FILLS + 2 * s + 1)
                                if s >= 4:
                                    act.wait_ge(sem("l_ready"), it * STEPS + s - 3)
                                sl = 2 * s % 3
                                nc.scalar.copy(ASB[s % 4][:, :], bank(2 * sl, 2)).then_inc(sem("a_copied_act"), 1)
                        if n >= 1:
                            exponential(n - 1)
                    exponential(NT - 1)

            norm_out(1)
            act.wait_ge(sem("router_psum0"), 1)
            A(sc[:, :, :], bank(4, 2).rearrange("p (t e) -> p t e", e=E0), ACT.Sigmoid).then_inc(sem("scores0_ready"), 1)

            def moe(l):
                m = MOE[l]
                nb, npro = m["n_body"], m["n_pro"]

                def run(seq, base, first=False):
                    for k in range(len(seq)):
                        act.wait_ge(sem(f"gu_done{l}"), base + k + 1)
                        if not (first and k < 2):
                            act.wait_ge(sem(f"su_done{l}"), base + k - 1)
                        A(SL[k % 2][:, :], bank(2 * (k % 2)), ACT.Silu).then_inc(sem(f"silu_done{l}"), 1)

                if l == 0:
                    run(m["pro"], 0, first=True)
                    with act.Fori(0, m["halves"] // 2) as it:
                        run(m["body"], npro + it * nb)
                else:
                    run(m["body"], 0, first=True)
                    with act.Fori(1, m["halves"] // 2) as it:
                        run(m["body"], it * nb)
                total = npro + nb * m["halves"] // 2
                act.wait_ge(sem(f"down_done{l}"), total)
                for q in range(NC):
                    nc.scalar.copy(YT[:, q * CH:(q + 1) * CH], bank(4 + q)).then_inc(sem("yt_ready"), 1)

            moe(0)
            norm_out(2)
            act.wait_ge(sem("logits_ready"), 1)
            A(TS[:, :, 64:96], TS[:, :, 64:96], ACT.Exp).then_inc(sem("exps_ready"), 1)
            act.wait_ge(sem("ts_psum"), 1)
            nc.scalar.copy(TI[:, :], PS[0:64, 0:T]).then_inc(sem("ti_ready"), 1)
            nc.scalar.copy(TW[64:96, :], PS[64:96, 0:T]).then_inc(sem("ti_ready"), 1)
            for m, f in ((0, 3), (1, 8)):
                act.wait_ge(sem("expand_psum"), f)
                if m == 1:
                    act.wait_ge(sem("expanded_dve"), 3)
                nc.scalar.copy(WE[:, :], bank(4 if (f - 1) % 2 == 0 else 0, 4)).then_inc(sem("expanded_act"), 1)

            norm_out(3)
            act.wait_ge(sem("router1_ready"), 1)
            A(sc[:, :, 0:E1], sc[:, :, 0:E1], ACT.Exp).then_inc(sem("scores1_ready"), 1)
            moe(1)

        @block.gpsimd
        def _(pool):
            gp = nc.gpsimd

            def norm_scale(l):
                pool.wait_ge(sem("moments_ready"), l + 1)
                gp.tensor_scalar(rstd[:, :], moments[:, :, 1], EPS, None, ALU.add).then_inc(sem("var_ready"), 1)
                pool.wait_ge(sem("var_ready"), l + 1)
                gp.tensor_tensor(rstd[:, :], rstd[:, :], half[:, :], ALU.pow).then_inc(sem("rstd_ready"), 1)

            gp.memset(half[:, :], -0.5).then_inc(sem("pool_zero"), 1)
            gp.memset(VS[:, :, :, 16:32], 0.0).then_inc(sem("pool_zero"), 1)
            gp.memset(hxy[:, :, :, :], 0.0).then_inc(sem("pool_zero"), 1)
            gp.memset(MR[:, :, :, :], 0.0).then_inc(sem("pool_zero"), 1)
            pool.wait_ge(sem("pool_zero"), 2)
            gp.memset(VS[:, :, :, 16:17], 1.0).then_inc(sem("pool_zero"), 1)
            norm_scale(0)
            pool.wait_ge(sem("xn_ready"), NC)
            gp.tensor_tensor(XS[:, :, :], X[:, :, :], XN[:, :, :], ALU.add).then_inc(sem("xs_ready"), 1)
            for g in range(G):
                pool.wait_ge(sem("f_ready"), 3 + g)
                gp.tensor_scalar(F[4 + g][:, :], F[2 + g][:, :], 0.2, None, ALU.mult).then_inc(sem("f_scaled"), 1)
            pool.wait_ge(sem("q_final"), 4)
            for g in range(G):
                with pool.Fori(0, NC) as c:
                    it = c + g * NC
                    pool.wait_ge(sem("q_used"), it + 1)
                    gp.tensor_copy(QSA[:, :], QA[g][:, ds(c * CH, CH)])
                    gp.tensor_copy(QSB[:, :], QB[g][:, ds(c * CH, CH)]).then_inc(sem("q_staged"), 1)

            def moe(l):
                m = MOE[l]
                nb, npro, sub = m["n_body"], m["n_pro"], m["sub"]

                def run(seq, base, it=None, first=False):
                    for k, (slot, c) in enumerate(seq):
                        h, s = divmod(slot, sub)
                        if it is not None and c == 0 and s == 0:
                            per = len(SEGMENTS0) if l == 0 else 1
                            pool.wait_ge(sem(f"m_loaded{l}_{h}"), (it + 1) * 16 * per)
                        pool.wait_ge(sem(f"su_done{l}"), base + k + 1)
                        if not (first and k < 2):
                            pool.wait_ge(sem(f"down_done{l}"), base + k - 1)
                        if it is None:
                            ins = gp.tensor_copy(HB[k % 2][:, :], SU[k % 2][:, :])
                        else:
                            mask = MK[:, h, s if l == 0 else 0, c * CH:(c + 1) * CH]
                            ins = gp.tensor_tensor(HB[k % 2][:, :], SU[k % 2][:, :], mask, ALU.mult)
                        ins.then_inc(sem(f"h_ready{l}"), 1)

                if l == 0:
                    run(m["pro"], 0, first=True)
                    with pool.Fori(0, m["halves"] // 2) as it:
                        run(m["body"], npro + it * nb, it)
                else:
                    run(m["body"], 0, 0, first=True)
                    with pool.Fori(1, m["halves"] // 2) as it:
                        run(m["body"], it * nb, it)

            norm_scale(1)
            moe(0)
            norm_scale(2)
            pool.wait_ge(sem("x_moe0"), NC)
            gp.tensor_tensor(XS[:, :, :], X[:, :, :], boutb[:, :].unsqueeze(1).to_broadcast([P, NT, P]),
                             ALU.add).then_inc(sem("xs_ready"), 1)
            norm_scale(3)
            moe(1)

        @block.vector
        def _(dve):
            v = nc.vector
            TS_, TT, STT = v.tensor_scalar, v.tensor_tensor, v.scalar_tensor_tensor

            def after(ins, name, n):
                ins.then_inc(sem(name), 1)
                dve.wait_ge(sem(name), n)

            def norm(l):
                for t in range(NT):
                    last = v.bn_stats(stats[:, t, :], X[:, t, :])
                after(last, "stats_ready", l + 1)
                for t in range(NT):
                    last = v.bn_aggr(moments[:, t, :], stats[:, t, :])
                after(last, "moments_ready", l + 1)
                dve.wait_ge(sem("rstd_ready"), l + 1)
                for t in range(NT):
                    last = TS_(XN[:, t, :], X[:, t, :], moments[:, t, 0:1], rstd[:, t:t + 1], ALU.subtract, ALU.mult)
                    if t % 4 == 3:
                        last.then_inc(sem("xn_ready"), 1)

            dve.wait_ge(sem("x_loaded"), 16)
            norm(0)
            dve.wait_ge(sem("cb_loaded"), 16)
            dve.wait_ge(sem("cf_loaded"), 16)
            v.tensor_copy(CB[:, :], YT[:, 0:NB]).then_inc(sem("cb_ready"), 1)

            dve.wait_ge(sem("qkv_loaded"), 64)
            for i in range(4):
                dve.wait_ge(sem("proj_done"), i + 1)
                TS_(F[i][:, :], bank(4 * ((i + 1) % 2), 4), bqk[:, i:i + 1], 1.0 if i < 2 else 1 / math.sqrt(DQK),
                    ALU.add, ALU.mult).then_inc(sem("f_ready"), 1)
            dve.wait_ge(sem("v_psum"), 1)
            dve.wait_ge(sem("pool_zero"), 5)
            TT(VS[:, :, :, 0:DV], bank(4, 4).rearrange("p (t h d) -> p t h d", h=H, d=DV),
               bvb[:, :].rearrange("p (h d) -> p h d", d=DV).unsqueeze(1).to_broadcast([P, NT, H, DV]),
               ALU.add).then_inc(sem("v_ready"), 1)
            targets = [KS[0], KS[1], QA[0], QA[1], QB[0], QB[1]]

            def split(i):
                sel = cf("ksel") if i < 2 else cf("qsel")
                if i in (2, 3):
                    dve.wait_ge(sem("f_scaled"), i - 1)
                dve.wait_ge(sem("part_ready"), 2 * i + 1)
                STT(F[i][:, :], TB[i % 3][:, :], sel[:, 0:1], F[i][:, :], ALU.mult, ALU.add).then_inc(sem("rest1_ready"), 1)
                dve.wait_ge(sem("part_ready"), 2 * i + 2)
                STT(targets[i][:, :], TB[i % 3][:, :], sel[:, 1:2], F[i][:, :], ALU.mult, ALU.add).then_inc(sem("split_ready"), 1)

            split(0)
            split(1)
            split(2)
            split(3)
            for h in range(H):
                dve.wait_ge(sem("extent_psum"), h + 1)
                last = v.reduce_max(hm[:, h:h + 1], bank(4 * (h % 2), 4), AX.X)
                last.then_inc(sem("extent_ready"), 1)
            dve.wait_ge(sem("extent_ready"), H)
            for d in range(DQK):
                last = v.tensor_copy(hxy[:, :, d, :].rearrange("p g (j r) -> p g j r", r=32)[:, :, :, 9 * d:9 * d + 9],
                                     hm[:, :].rearrange("p (g j) -> p g j", g=G).unsqueeze(3).to_broadcast([P, G, HG, 9]))
            last.then_inc(sem("hxy_ready"), 1)
            dve.wait_ge(sem("corners_psum"), 1)
            after(v.tensor_copy(vtx[:, :], PS[:, 0:G * P]), "corner_step", 1)
            after(v.tensor_copy(vtb[:, :], vtx[:, :]), "corner_step", 2)
            after(STT(vtx[:, :], vtb[:, :], cf("ksel")[:, 0:1], vtx[:, :], ALU.mult, ALU.add), "corner_step", 3)
            after(v.tensor_copy(vtb[:, :], vtx[:, :]), "corner_step", 4)
            STT(VV[:, :], vtb[:, :], cf("ksel")[:, 1:2], vtx[:, :], ALU.mult, ALU.add).then_inc(sem("corners_ready"), 1)
            split(4)
            split(5)
            bound, neg, rest, tmp = (small[:, i, :] for i in range(4))
            for tp in range(NT // 2):
                dve.wait_ge(sem("bound_psum"), tp + 1)
                v.reduce_max(bound[:, tp * 16:(tp + 1) * 16],
                             bank(4 * (tp % 2), 4).rearrange("p (a b) -> p a b", b=P), AX.X).then_inc(sem("bound_ready"), 1)
            dve.wait_ge(sem("bound_ready"), NT // 2)
            after(STT(tmp, bound, 0.2, bound, ALU.mult, ALU.max), "max_step", 1)
            after(TS_(neg, tmp, -1.0, None, ALU.mult), "max_step", 2)
            after(v.tensor_copy(mparts[:, 0, :], neg), "max_step", 3)
            after(TT(rest, neg, mparts[:, 0, :], ALU.subtract), "max_step", 4)
            after(v.tensor_copy(mparts[:, 1, :], rest), "max_step", 5)
            after(TT(mparts[:, 2, :], rest, mparts[:, 1, :], ALU.subtract), "max_step", 6)
            mv = mparts[:, :, :].rearrange("p k (tp j g tt) -> p g tt tp j k", j=HG, g=G, tt=2)
            for g in range(G):
                o = MR[:, g, :, :].rearrange("p (tp tt) (j r) -> p tt tp j r", tt=2, r=32)
                for tt in range(2):
                    last = v.tensor_copy(o[:, tt, :, :, KROWS:KSC], mv[:, g, tt])
            last.then_inc(sem("mr_ready"), 1)
            for g in range(G):
                dve.wait_ge(sem("mrows_psum"), g + 1)
                for Q in (QA[g], QB[g]):
                    TT(Q[:, :], bank(4 * g, 4), Q[:, :], ALU.add).then_inc(sem("q_final"), 1)
            dve.sem_inc(sem("sums_taken"), 1)

            for g in range(G):
                with dve.Fori(0, NC) as c:
                    it = c + g * NC
                    for s in range(STEPS):
                        n, hp = divmod(s, 2)
                        if s in DVE_COPIES:
                            dve.wait_ge(sem("scores_done"), it * FILLS + 2 * s + 1)
                            v.tensor_copy(ASB[s % 4][:, :], bank(2 * (2 * s % 3), 2)).then_inc(sem("a_copied_dve"), 1)
                        name, rank, per = copied(s)
                        dve.wait_ge(sem(name), it * per + rank)
                        dve.wait_ge(sem("scores_done"), it * FILLS + 2 * s + 2)
                        if n >= 2 and hp == 0:
                            dve.wait_ge(sem("p_ready"), it * NT + n - 1)
                        TT(LB[n % 2][:, 2 * hp:2 * hp + 2, :],
                           bank(2 * ((2 * s + 1) % 3), 2).rearrange("p (j q) -> p j q", j=2),
                           ASB[s % 4][:, :].rearrange("p (j q) -> p j q", j=2), ALU.max).then_inc(sem("l_ready"), 1)
                    dve.wait_ge(sem("pv_done"), (it + 1) * NT)
                    v.tensor_copy(OT[g][:, ds(c * CH, CH)], bank(6)).then_inc(sem("sums_taken"), 1)

            dve.wait_ge(sem("rest_loaded"), 16 * 8)
            dve.wait_ge(sem("xs_ready"), 1)
            og = small[:, 0, :]
            for q in range(NC):
                dve.wait_ge(sem("o_psum"), q + 1)
                o = bank(2 * q, 2).rearrange("p (a b) -> p a b", b=32)
                ogq = og[:, q * 32:(q + 1) * 32]
                tq = YT[:, q * CH:(q + 1) * CH].rearrange("p (a b) -> p a b", b=DV)
                after(v.reciprocal(ogq, o[:, :, DV]), "o_step", 4 * q + 1)
                after(TS_(ogq, ogq, gam[:, 0:1], None, ALU.mult), "o_step", 4 * q + 2)
                after(TT(tq, o[:, :, 0:DV], ogq.unsqueeze(2).to_broadcast([P, 32, DV]), ALU.mult), "o_step", 4 * q + 3)
                after(TT(X[:, 4 * q:4 * q + 4, :], XS[:, 4 * q:4 * q + 4, :],
                         YT[:, q * CH:(q + 1) * CH].rearrange("p (t c) -> p t c", c=P), ALU.add), "o_step", 4 * q + 4)

            norm(1)

            def masks_out(l, n):
                dve.wait_ge(sem(f"mask_psum{l}"), 1)
                for q in range(NC):
                    v.tensor_copy(MT[0:n, q * CH:(q + 1) * CH], PS[0:n, q * BANK:(q + 1) * BANK]).then_inc(sem(f"mask_t{l}"), 1)

            def choose(l, n, k, scores, key):
                for t in range(NT):
                    last = v.max(top8[:, t, :], key[:, t, 0:n])
                after(last, f"top_step{l}", 1)
                after(v.memset(top8[:, :, k:8], -3e38), f"top_step{l}", 2)
                for t in range(NT):
                    last = v.match_replace(rp[:, t, 0:n], top8[:, t, :], key[:, t, 0:n], -1e30)
                after(last, f"top_step{l}", 3)
                after(TT(rp[:, :, 0:n], rp[:, :, 0:n], key[:, :, 0:n], ALU.not_equal), f"top_step{l}", 4)
                after(TT(scores[:, :, 0:n], scores[:, :, 0:n], rp[:, :, 0:n], ALU.mult), f"top_step{l}", 5)
                after(v.reduce_sum(rsum[:, :], scores[:, :, 0:n], AX.X), f"top_step{l}", 6)

            dve.wait_ge(sem("scores0_ready"), 1)
            after(TT(bs[:, :, :], sc[:, :, :], gb0[:, :].unsqueeze(1).to_broadcast([P, NT, E0]), ALU.add), "keys_ready", 1)
            choose(0, E0, TOP0, sc, bs)
            after(TS_(rsum[:, :], rsum[:, :], 1e-20, None, ALU.add), "top_step0", 7)
            after(v.reciprocal(rsum[:, :], rsum[:, :]), "top_step0", 8)
            after(TT(sc[:, :, :], sc[:, :, :], rsum[:, :].unsqueeze(2).to_broadcast([P, NT, E0]), ALU.mult), "top_step0", 9)
            TS_(sc[:, :, :], sc[:, :, :], SCALE0, None, ALU.mult).then_inc(sem("mask_ready0"), 1)
            masks_out(0, E0)

            def moe(l):
                m = MOE[l]
                nb, npro = m["n_body"], m["n_pro"]

                def run(seq, base, first=False):
                    for k in range(len(seq)):
                        dve.wait_ge(sem(f"silu_done{l}"), base + k + 1)
                        if not (first and k < 2):
                            dve.wait_ge(sem(f"h_ready{l}"), base + k - 1)
                        TT(SU[k % 2][:, :], bank(2 * (k % 2) + 1), SL[k % 2][:, :], ALU.mult).then_inc(sem(f"su_done{l}"), 1)

                if l == 0:
                    run(m["pro"], 0, first=True)
                    with dve.Fori(0, m["halves"] // 2) as it:
                        run(m["body"], npro + it * nb)
                else:
                    run(m["body"], 0, first=True)
                    with dve.Fori(1, m["halves"] // 2) as it:
                        run(m["body"], it * nb)
                for q in range(NC):
                    dve.wait_ge(sem("y_psum"), NC * l + q + 1)
                    last = v.tensor_copy(X[:, 4 * q:4 * q + 4, :], bank(q).rearrange("p (t c) -> p t c", c=P))
                    last.then_inc(sem(f"x_moe{l}"), 1)
                dve.wait_ge(sem(f"x_moe{l}"), NC)

            moe(0)
            norm(2)

            dve.wait_ge(sem("xt_ready"), 2 * NC + 1)
            TS_(dx[:, :], cf("amask"), XT[:, 0:1], None, ALU.mult).then_inc(sem("dx_ready"), 1)
            dve.wait_ge(sem("ol_psum"), 1)
            after(TT(OL[:, :, :], bank(4, 2).rearrange("p (t e) -> p t e", e=2 * HP),
                     bol[:, :].unsqueeze(1).to_broadcast([P, NT, 2 * HP]), ALU.add), "ol_ready", 1)
            lg = OL[:, :, HP:2 * HP].rearrange("p t (h k) -> p t h k", k=PT)
            wt = TS[:, :, 64:96].rearrange("p t (h k) -> p t h k", k=PT)
            after(v.reduce_max(lmax[:, :, :], lg, AX.X), "lk_step", 1)
            TT(wt, lg, lmax[:, :, :].unsqueeze(3).to_broadcast([P, NT, 8, PT]), ALU.subtract).then_inc(sem("logits_ready"), 1)
            off = OL[:, :, 0:HP]
            mag, frac, ng, idx = (i[:, :, :] for i in ix)
            after(STT(mag, off, -1.0, off, ALU.mult, ALU.max), "lk_step", 2)
            after(TS_(mag, mag, 300.0, None, ALU.min), "lk_step", 3)
            TS_(ng, off, -1.0, None, ALU.is_le)
            after(v.tensor_copy(iint[:, :, :], mag), "lk_step", 4)
            after(v.tensor_copy(frac, iint[:, :, :]), "lk_step", 5)
            after(TT(idx, frac, mag, ALU.is_gt), "lk_step", 6)
            after(TT(mag, frac, idx, ALU.subtract), "lk_step", 7)
            after(TS_(frac, mag, -2.0, float(P), ALU.mult, ALU.add), "lk_step", 8)
            after(TT(frac, frac, ng, ALU.mult), "lk_step", 9)
            after(TT(idx, mag, frac, ALU.add), "lk_step", 10)
            after(TS_(idx, idx, 0.0, P - 1.0, ALU.max, ALU.min), "lk_step", 11)
            hi = TS[:, :, 32:64]
            after(TS_(mag, idx, 1 / 16, None, ALU.mult), "lk_step", 12)
            after(v.tensor_copy(iint[:, :, :], mag), "lk_step", 13)
            after(v.tensor_copy(frac, iint[:, :, :]), "lk_step", 14)
            after(TT(ng, frac, mag, ALU.is_gt), "lk_step", 15)
            after(TT(hi, frac, ng, ALU.subtract), "lk_step", 16)
            after(TS_(mag, hi, -16.0, None, ALU.mult), "lk_step", 17)
            TT(TS[:, :, 0:32], mag, idx, ALU.add)
            dve.wait_ge(sem("exps_ready"), 1)
            after(v.reduce_sum(lmax[:, :, :], wt, AX.X), "lk_step", 18)
            after(v.reciprocal(lmax[:, :, :], lmax[:, :, :]), "lk_step", 19)
            TT(wt, wt, lmax[:, :, :].unsqueeze(3).to_broadcast([P, NT, 8, PT]), ALU.mult).then_inc(sem("ts_ready"), 1)
            dve.wait_ge(sem("tables_psum"), 1)
            v.tensor_copy(cw[:, :], PS[:, 7 * BANK:7 * BANK + P])
            after(v.memset(BD[:, :, :], 0.0), "lk_step", 20)
            for k in range(2):
                last = TT(BD[:, k, 64 * k:64 * k + 64].rearrange("p (h q) -> p h q", q=8),
                          PS[:, 7 * BANK + P:7 * BANK + P + 8].unsqueeze(1).to_broadcast([P, 8, 8]),
                          cf("bdmask").rearrange("p (h q) -> p h q", q=8), ALU.mult)
            last.then_inc(sem("tables_ready"), 1)
            for m in range(2):
                for k in range(2):
                    f = 5 * m + k
                    dve.wait_ge(sem("expand_psum"), f + 1)
                    TS_(OH[k][:, :], bank(4 if f % 2 == 0 else 0, 4), cf("bval"), None, ALU.is_equal).then_inc(sem("expanded_dve"), 1)
                f = 5 * m + 3
                dve.wait_ge(sem("expand_psum"), f + 1)
                dve.wait_ge(sem("expanded_act"), m + 1)
                STT(AW[:, :], bank(4 if f % 2 == 0 else 0, 4), cf("aval"), WE[:, :], ALU.is_equal, ALU.mult).then_inc(
                    sem("expanded_dve"), 1)
                f += 1
                dve.wait_ge(sem("expand_psum"), f + 1)
                dve.wait_ge(sem("expanded_dve"), 4 * m + 3)
                TT(PR[m][:, :], bank(4 if f % 2 == 0 else 0, 4), AW[:, :], ALU.mult).then_inc(sem("expanded_dve"), 1)
            dve.wait_ge(sem("xs_ready"), 2)
            for q in range(NC):
                dve.wait_ge(sem("lookup_psum"), q + 1)
                last = TT(X[:, 4 * q:4 * q + 4, :], XS[:, 4 * q:4 * q + 4, :],
                          bank(4 + q).rearrange("p (t c) -> p t c", c=P), ALU.add)
            after(last, "x_lookup", 1)

            norm(3)
            dve.wait_ge(sem("router_psum1"), 1)
            lg = PS[:, 4 * BANK:4 * BANK + NT * E1].rearrange("p (t e) -> p t e", e=E1)
            after(v.reduce_max(rsum[:, :], lg, AX.X), "r1_step", 1)
            TT(sc[:, :, 0:E1], lg, rsum[:, :].unsqueeze(2).to_broadcast([P, NT, E1]), ALU.subtract).then_inc(sem("router1_ready"), 1)
            dve.wait_ge(sem("scores1_ready"), 1)
            after(v.reduce_sum(rsum[:, :], sc[:, :, 0:E1], AX.X), "r1_step", 2)
            after(v.reciprocal(rsum[:, :], rsum[:, :]), "r1_step", 3)
            after(TT(sc[:, :, 0:E1], sc[:, :, 0:E1], rsum[:, :].unsqueeze(2).to_broadcast([P, NT, E1]), ALU.mult), "r1_step", 4)
            after(v.tensor_copy(bs[:, :, 0:E1], sc[:, :, 0:E1]), "r1_step", 5)
            choose(1, E1, TOP1, sc, bs)
            after(v.reciprocal(rsum[:, :], rsum[:, :]), "r1_step", 6)
            TT(sc[:, :, 0:E1], sc[:, :, 0:E1], rsum[:, :].unsqueeze(2).to_broadcast([P, NT, E1]), ALU.mult).then_inc(sem("mask_ready1"), 1)
            masks_out(1, E1)
            moe(1)


_OUT_SHAPE = (1, T, P)


def _layout(i):
    f = {k: np.asarray(v) for k, v in i.items()}
    d = {"x": f["L0_attn_x"].reshape(T, P), "consts": constants()}
    wqk, bqk = np.zeros((P, 4, P), np.float32), np.zeros((P, 4), np.float32)
    for n, w, b in ((0, f["L0_attn_Wk"], f["L0_attn_bk"]), (2, f["L0_attn_Wq"], f["L0_attn_bq"])):
        for h in range(H):
            g, j = divmod(h, HG)
            for r in range(KROWS):
                wqk[:, n + g, 32 * j + r] = w[DQK * h + r // 9]
                bqk[32 * j + r, n + g] = b[DQK * h + r // 9]
            if n == 0:
                bqk[32 * j + KROWS:32 * j + KSC, g] = 1.0
    d["wqk"], d["bqk"] = wqk, bqk
    d["wvt"] = f["L0_attn_Wv"].T
    d["bv"], d["gamma"] = f["L0_attn_bv"], f["L0_attn_gamma"]
    d["gw0"], d["gb0"] = f["L0_ffn_gate_w"], f["L0_ffn_gate_bias"]

    def weights(gate, up, down, halves):
        parts = [gate.reshape(P, halves, -1, P), up.reshape(P, halves, -1, P),
                 down.reshape(halves, -1, P, P).transpose(2, 0, 1, 3)]
        return np.concatenate(parts, 3).transpose(1, 0, 2, 3)

    g0 = f["L0_ffn_all_gate_proj"].transpose(1, 0, 2).reshape(P, -1)
    u0 = f["L0_ffn_all_up_proj"].transpose(1, 0, 2).reshape(P, -1)
    d["w0"] = weights(g0, u0, f["L0_ffn_all_down_proj"].reshape(-1, P), HALVES0)
    pad = 2 * P - f["L0_ffn_sh_gate"].shape[1]
    d["wsh"] = weights(np.pad(f["L0_ffn_sh_gate"], ((0, 0), (0, pad))), np.pad(f["L0_ffn_sh_up"], ((0, 0), (0, pad))),
                       np.pad(f["L0_ffn_sh_down"], ((0, pad), (0, 0))), 1)[0]
    d["wol"] = np.concatenate([f["L1_attn_W_off"][:, 0::2], f["L1_attn_W_attn"]], 1)
    d["bol"] = np.concatenate([f["L1_attn_b_off"][0::2], f["L1_attn_b_attn"]])
    d["wout"], d["bout"] = f["L1_attn_W_out"], f["L1_attn_b_out"]
    d["gw1"] = f["L1_ffn_gate_w"].T
    gu = f["L1_ffn_gate_up_proj"].reshape(E1, 2, -1, P)
    d["w1"] = weights(gu[:, 0].transpose(2, 0, 1).reshape(P, -1), gu[:, 1].transpose(2, 0, 1).reshape(P, -1),
                      f["L1_ffn_down_proj"].transpose(0, 2, 1).reshape(-1, P), HALVES1)
    return {k: np.ascontiguousarray(v, np.float32) for k, v in d.items()}


def kernel(**inputs):
    import concourse.bacc as bacc
    from concourse.bass_utils import run_bass_kernel_spmd as run

    nc = bacc.Bacc("TRN2", target_bir_lowering=False, num_devices=1)
    arrays, args = {}, {}
    for name, v in _layout(inputs).items():
        arrays[f"in_{name}"] = v
        args[name] = nc.dram_tensor(f"in_{name}", v.shape, mybir.dt.float32, kind="ExternalInput").ap()
    out = nc.dram_tensor("out_0", (T, P), mybir.dt.float32, kind="ExternalOutput").ap()
    build(nc, args, out)
    r = run(nc, [arrays], core_ids=[0])
    return r.results[0]["out_0"].reshape(_OUT_SHAPE)
```

```python
import math
from contextlib import ExitStack

import concourse.bass as bass
import numpy as np
from concourse import mybir

P = 128
T = 2048
NT = T // P
BANK = 512
CH = 512
NC = T // CH
H = 8
DQK, DV = 2, 16
G = 2
HG = H // G
KROWS = 9 * DQK
KSC = KROWS + 3
EPS = 1e-5
E0, TOP0, SCALE0 = 64, 6, 2.5
E1, TOP1 = 8, 2
HP, PT = 32, 4
SUB0 = 3
SUB1 = 4
HALVES0 = E0 * 96 // P // SUB0
HALVES1 = E1
SEGMENTS0 = [(s, p0, p1, e) for s in range(SUB0) for e in range(4)
             for p0, p1 in [(max(96 * e - 128 * s, 0), min(96 * (e + 1) - 128 * s, 128))] if p0 < p1]

F32_COLS = [("ident", P), ("ksel", 2), ("qsel", 2), ("bval", 1), ("aval", 1), ("hmask", HG), ("selx", P), ("amask", 8),
            ("bdmask", 64), ("vx", P), ("vy", P), ("ones", P), ("selw", 2 * P)]
BF_COLS = [("identb", P), ("ud", P), ("selb", 4 * P), ("sela", 2 * P)]


def columns(cols):
    at, out = 0, {}
    for name, n in cols:
        out[name] = (at, at + n)
        at += n
    return out, at


FC, NF = columns(F32_COLS)
BC, NB = columns(BF_COLS)


def constants():
    c = {}
    p = np.arange(P)
    c["ident"] = c["identb"] = np.eye(P)
    row = p % 32
    k_part = np.where(row < KROWS, row % 3, 0)
    q_part = np.where(row < KROWS, row % 9 // 3, 0)
    c["ksel"] = -np.stack([k_part >= 1, k_part >= 2], 1).astype(float)
    c["qsel"] = -np.stack([q_part >= 1, q_part >= 2], 1).astype(float)
    c["bval"] = (p % 16)[:, None]
    c["aval"] = (p % 8)[:, None]
    c["hmask"] = p[:, None] // 32 == np.arange(HG)[None, :]
    c["selx"] = p[:, None] % 16 == p[None, :] % 16
    c["amask"] = p[:, None] // 16 == np.arange(8)[None, :]
    c["bdmask"] = np.repeat(p[:, None] // 16 == np.arange(8)[None, :], 8, axis=1)
    angle = 2 * np.pi * p / P
    u = np.stack([np.cos(angle), np.sin(angle)], 1).astype(np.float32)
    u = ((u.view(np.uint32) + 0x8000) & 0xFFFF0000).astype(np.uint32).view(np.float32).astype(np.float64)
    ud = np.zeros((P, P))
    for h in range(HG):
        for d in range(DQK):
            for j in range(3):
                ud[32 * h + 9 * d + j] = u[:, d]
    c["ud"] = ud
    nxt = (p + 1) % P
    inv = np.linalg.inv(np.stack([u, u[nxt]], 1))
    for name, d in (("vx", 0), ("vy", 1)):
        m = np.zeros((P, P))
        m[p, p] = inv[:, d, 0]
        m[nxt, p] = inv[:, d, 1]
        c[name] = m
    c["ones"] = np.ones((P, P))
    selw, sela, selb = np.zeros((P, 2, P)), np.zeros((P, 2, P)), np.zeros((P, 4, P))
    for m in range(2):
        selw[64 + 16 * m + p // 8, m, p] = 1
        sela[32 + 16 * m + p // 8, m, p] = 1
    for k in range(4):
        selb[8 * k + p // 16, k, p] = 1
    c["selw"], c["sela"], c["selb"] = selw.reshape(P, -1), sela.reshape(P, -1), selb.reshape(P, -1)
    return np.concatenate([np.asarray(c[n], np.float32) for n, _ in F32_COLS + BF_COLS], 1)


def build(nc, a, out):
    f32, bf16, f32r = mybir.dt.float32, mybir.dt.bfloat16, mybir.dt.float32r
    ALU, ACT, AX = mybir.AluOpType, mybir.ActivationFunctionType, mybir.AxisListType
    ds = bass.ds

    mask0_dram = nc.dram_tensor("mask0_scratch", (E0, T), f32, kind="Internal").ap()
    mask1_dram = nc.dram_tensor("mask1_scratch", (E1, T), f32, kind="Internal").ap()

    ctx = ExitStack()
    with ctx:
        def sb(name, shape, dt=f32, stack=ctx):
            return stack.enter_context(nc.sbuf_tensor(name, shape, dt))

        sems = {}

        def sem(name):
            if name not in sems:
                sems[name] = ctx.enter_context(nc.semaphore(name))
            return sems[name]

        CF = sb("CF", [P, NF])
        CB = sb("CB", [P, NB], bf16)
        X = sb("X", [P, NT, P])
        XN = sb("XN", [P, NT, P])
        XS = sb("XS", [P, NT, P])
        XT = sb("XT", [P, T])
        YT = sb("YT", [P, T])
        WR = sb("WR", [P, 2 * SUB1, 3 * P])
        stats = sb("stats", [P, NT, 6])
        moments = sb("moments", [P, NT, 2])
        rstd = sb("rstd", [P, NT])
        half = sb("half", [P, NT])
        wvt = sb("wvt", [P, P])
        bvb = sb("bvb", [P, P])
        wqk = sb("wqk", [P, 4, P])
        bqk = sb("bqk", [P, 4])
        gam = sb("gam", [P, 1])
        gw0 = sb("gw0", [P, E0])
        gb0 = sb("gb0", [P, E0])
        wol = sb("wol", [P, 2 * HP])
        bol = sb("bol", [P, 2 * HP])
        wout = sb("wout", [P, P])
        boutb = sb("boutb", [P, P])
        gw1 = sb("gw1", [P, E1])
        small = sb("small", [P, 8, NT * H])
        PS = ctx.enter_context(nc.psum_tensor("PS", [P, 8 * BANK], f32))

        def cf(name, lo=0, hi=None):
            s, e = FC[name]
            return CF[:, s + lo:(s + hi if hi else e)]

        def cb(name, lo=0, hi=None):
            s, e = BC[name]
            return CB[:, s + lo:(s + hi if hi else e)]

        def bank(b, n=1):
            return PS[:, b * BANK:(b + n) * BANK]

        att = ExitStack()
        KS = [sb(f"KS{g}", [P, T], bf16, att) for g in range(G)]
        QA = [sb(f"QA{g}", [P, T], bf16, att) for g in range(G)]
        QB = [sb(f"QB{g}", [P, T], bf16, att) for g in range(G)]
        VS = sb("VS", [P, NT, H, 32], f32, att)
        OT = [sb(f"OT{g}", [P, T], f32, att) for g in range(G)]
        pre = ExitStack()
        F = [sb(f"F{i}", [P, T], f32, pre) for i in range(6)]
        TB = [sb(f"TB{i}", [P, T], bf16, pre) for i in range(3)]
        hm = sb("hm", [P, H], f32, pre)
        hxy = sb("hxy", [P, G, 2, P], f32, pre)
        vtx = sb("vtx", [P, G * P], f32, pre)
        vtb = sb("vtb", [P, G * P], bf16, pre)
        VV = sb("VV", [P, G * P], bf16, pre)
        mparts = sb("mparts", [P, 3, NT * H], bf16, pre)
        MR = sb("MR", [P, G, NT, P], bf16, pre)
        pre.close()
        flow = ExitStack()
        ASB = [sb(f"ASB{i}", [P, 2 * CH], f32, flow) for i in range(2)]
        KP = [sb(f"KP{j}", [P, T], bf16, flow) for j in range(HG)]
        LB = [sb(f"LB{i}", [P, HG, CH], f32, flow) for i in range(2)]
        PB = [sb(f"PB{i}", [P, HG, CH], f32, flow) for i in range(2)]
        QSA = sb("QSA", [P, CH], bf16, flow)
        QSB = sb("QSB", [P, CH], bf16, flow)
        flow.close()
        att.close()
        weight_mem = ExitStack()
        WH = sb("WH", [P, 2 * SUB1, 3 * P], f32r, weight_mem)
        WL = sb("WL", [P, 2 * SUB1, 3 * P], f32r, weight_mem)
        moe_mem = ExitStack()
        XH = sb("XH", [P, T], f32r, moe_mem)
        XL = sb("XL", [P, T], f32r, moe_mem)
        MK = sb("MK", [P, 2, SUB0, T], f32, moe_mem)
        SL = [sb(f"SL{i}", [P, CH], f32, moe_mem) for i in range(2)]
        SU = [sb(f"SU{i}", [P, CH], f32, moe_mem) for i in range(2)]
        HF = [sb(f"HF{i}", [P, CH], f32, moe_mem) for i in range(2)]
        top8 = sb("top8", [P, NT, 8], f32, moe_mem)
        rsum = sb("rsum", [P, NT], f32, moe_mem)
        hidden = ExitStack()
        HH = [sb(f"HH{i}", [P, CH], f32r, hidden) for i in range(4)]
        HL = [sb(f"HL{i}", [P, CH], f32r, hidden) for i in range(4)]
        hidden.close()
        sc = sb("sc", [P, NT, E0], f32, moe_mem)
        bs = sb("bs", [P, NT, E0], f32, moe_mem)
        rp = sb("rp", [P, NT, E0], f32, moe_mem)
        MT = YT
        moe_mem.close()
        lk = ExitStack()
        OL = sb("OL", [P, NT, 2 * HP], f32, lk)
        TS = sb("TS", [P, NT, 3 * HP], f32, lk)
        ix = [sb(f"ix{i}", [P, NT, HP], f32, lk) for i in range(4)]
        iint = sb("iint", [P, NT, HP], mybir.dt.int32, lk)
        lmax = sb("lmax", [P, NT, 8], f32, lk)
        TI = sb("TI", [2 * HP, T], bf16, lk)
        TW = sb("TW", [3 * HP, T], f32, lk)
        OH = [sb(f"OH{i}", [P, T], f32, lk) for i in range(2)]
        WE = sb("WE", [P, T], f32, lk)
        AW = sb("AW", [P, T], f32, lk)
        PR = [sb(f"PR{i}", [P, T], f32, lk) for i in range(2)]
        dx = sb("dx", [P, 8], f32, lk)
        BD = sb("BD", [P, 2, P], f32, lk)
        cw = sb("cw", [P, P], f32, lk)
        lk.close()
        weight_mem.close()

        block = ctx.enter_context(nc.Block())

        STEPS = 2 * NT
        DVE_COPIES = [s for s in range(STEPS) if s % 4 == 2]
        ACT_COPIES = [s for s in range(STEPS) if s not in DVE_COPIES]
        FILLS = 2 * STEPS

        def copied(s):
            if s in DVE_COPIES:
                return "a_copied_dve", DVE_COPIES.index(s) + 1, len(DVE_COPIES)
            return "a_copied_act", ACT_COPIES.index(s) + 1, len(ACT_COPIES)

        def units(slots):
            return [(s, c) for s in slots for c in range(NC)]

        MOE = {
            0: dict(sub=SUB0, halves=HALVES0, pro=units([SUB0 * 2 - 2, SUB0 * 2 - 1])),
            1: dict(sub=SUB1, halves=HALVES1, pro=[]),
        }
        for m in MOE.values():
            m["body"] = units(range(2 * m["sub"]))
            m["n_body"] = len(m["body"])
            m["n_pro"] = len(m["pro"])

        def splits(m, k):
            return [(half, (k - start) // 2, start - 4) for half, start in ((1, 4), (0, m["n_body"] // 2 + 4))
                    if start <= k < start + 2 * m["sub"] and (k - start) % 2 == 0]

        @block.sync
        def _(sp):
            def load(dst, src, name="loaded"):
                sp.dma_start(dst, src).then_inc(sem(name), 16)

            load(X[:, :, :], a["x"].rearrange("(t p) c -> p t c", p=P), "x_loaded")
            load(CF[:, :], a["consts"][:, 0:NF], "cf_loaded")
            load(YT[:, 0:NB], a["consts"][:, NF:NF + NB], "cb_loaded")
            load(wqk[:, :, :], a["wqk"], "qkv_loaded")
            load(bqk[:, :], a["bqk"], "qkv_loaded")
            load(wvt[:, :], a["wvt"], "qkv_loaded")
            load(bvb[:, :], a["bv"].partition_broadcast(P), "qkv_loaded")
            load(gam[:, :], a["gamma"].partition_broadcast(P), "rest_loaded")
            load(gw0[:, :], a["gw0"], "rest_loaded")
            load(gb0[:, :], a["gb0"].partition_broadcast(P), "rest_loaded")
            load(wol[:, :], a["wol"], "rest_loaded")
            load(bol[:, :], a["bol"].partition_broadcast(P), "rest_loaded")
            load(wout[:, :], a["wout"], "rest_loaded")
            load(boutb[:, :], a["bout"].partition_broadcast(P), "rest_loaded")
            load(gw1[:, :], a["gw1"], "rest_loaded")

            def load_weights(l, it, h, weights):
                sub = MOE[l]["sub"]
                sp.dma_start(WR[:, h * sub:(h + 1) * sub, :], weights[ds(it * 2 + h, 1)].squeeze(0)).then_inc(
                    sem(f"w_loaded{l}_{h}"), 16)

            def load_masks(l, it, h, mask_dram):
                k = it * 2 + h
                if l == 0:
                    for s, p0, p1, e in SEGMENTS0:
                        sp.dma_start(MK[p0:p1, h, s, :], mask_dram[ds(k * 4 + e, 1), :].to_broadcast([p1 - p0, T])
                                     ).then_inc(sem(f"m_loaded{l}_{h}"), 16)
                else:
                    sp.dma_start(MK[:, h, 0, :], mask_dram[ds(k, 1), :].to_broadcast([P, T])
                                 ).then_inc(sem(f"m_loaded{l}_{h}"), 16)

            def moe_loads(l, weights, mask_dram):
                m = MOE[l]
                sub, nb, npro, n = m["sub"], m["n_body"], m["n_pro"], m["halves"] // 2
                load_masks(l, 0, 0, mask_dram)
                load_masks(l, 0, 1, mask_dram)
                with sp.Fori(1, n) as it:
                    for h in range(2):
                        sp.wait_ge(sem(f"w_split{l}_{h}"), it * sub)
                        load_weights(l, it, h, weights)
                    for h in range(2):
                        sp.wait_ge(sem(f"h_ready{l}"), npro + (it - 1) * nb + (h + 1) * nb // 2)
                        load_masks(l, it, h, mask_dram)
                sp.sem_inc(sem(f"w_loaded{l}_0"), 16)

            sp.dma_start(WR[:, 2 * SUB0 - 2:2 * SUB0, :], a["wsh"]).then_inc(sem("wsh_loaded"), 16)
            load_weights(0, 0, 0, a["w0"])
            sp.wait_ge(sem("wsh_split"), 2)
            load_weights(0, 0, 1, a["w0"])
            sp.wait_ge(sem("mask_t0"), 4)
            sp.dma_start(mask0_dram[:, :], MT[0:E0, :]).then_inc(sem("mask_stored0"), 16)
            sp.wait_ge(sem("mask_stored0"), 16)
            moe_loads(0, a["w0"], mask0_dram)

            for h in range(2):
                sp.wait_ge(sem(f"w_split0_{h}"), (HALVES0 // 2 + 1 - h) * SUB0)
            load_weights(1, 0, 0, a["w1"])
            load_weights(1, 0, 1, a["w1"])
            sp.wait_ge(sem("mask_t1"), 4)
            sp.dma_start(mask1_dram[:, :], MT[0:E1, :]).then_inc(sem("mask_stored1"), 16)
            sp.wait_ge(sem("mask_stored1"), 16)
            moe_loads(1, a["w1"], mask1_dram)

            for q in range(NC):
                sp.wait_ge(sem("x_moe1"), q + 1)
                sp.dma_start(out[q * CH:(q + 1) * CH, :].rearrange("(t p) c -> p t c", p=P),
                             X[:, 4 * q:4 * q + 4, :]).then_inc(sem("stored"), 16)
            sp.wait_ge(sem("stored"), 16 * NC)

        @block.tensor
        def _(pe):
            mm = nc.tensor.matmul
            ident = cf("ident")

            def transpose_norm(l):
                for q in range(NC):
                    pe.wait_ge(sem("xn_ready"), NC * l + q + 1)
                    for t in range(4 * q, 4 * q + 4):
                        last = nc.tensor.transpose(PS[:, t * P:(t + 1) * P], XN[:, t, :], ident)
                    last.then_inc(sem("xt_psum"), 1)

            pe.wait_ge(sem("cf_loaded"), 16)
            transpose_norm(0)

            pe.wait_ge(sem("xt_ready"), NC)
            pe.wait_ge(sem("qkv_loaded"), 64)
            for i in range(4):
                if i >= 2:
                    pe.wait_ge(sem("f_ready"), i - 1)
                for c in range(NC):
                    last = mm(bank(4 * ((i + 1) % 2) + c), wqk[:, i, :], XT[:, c * CH:(c + 1) * CH], start=True, stop=True)
                last.then_inc(sem("proj_done"), 1)
            pe.wait_ge(sem("f_ready"), 3)
            for t in range(NT):
                last = mm(PS[:, 4 * BANK + t * P:4 * BANK + (t + 1) * P], XT[:, t * P:(t + 1) * P], wvt[:, :], start=True, stop=True)
            last.then_inc(sem("v_psum"), 1)

            pe.wait_ge(sem("cb_ready"), 1)
            for h in range(H):
                g, j = divmod(h, HG)
                if j == 0:
                    pe.wait_ge(sem("split_ready"), g + 1)
                if h == 0:
                    pe.wait_ge(sem("f_ready"), 4)
                elif h == 1:
                    pe.wait_ge(sem("v_ready"), 1)
                else:
                    pe.wait_ge(sem("extent_ready"), h - 1)
                r = slice(32 * j, 32 * j + KROWS)
                for c in range(NC):
                    last = mm(bank(4 * (h % 2) + c), cb("ud")[r, :], KS[g][r, c * CH:(c + 1) * CH], start=True, stop=True)
                last.then_inc(sem("extent_psum"), 1)
            pe.wait_ge(sem("hxy_ready"), 1)
            for g in range(G):
                mm(PS[:, g * P:(g + 1) * P], hxy[:, g, 0, :], cf("vx"), start=True, stop=False)
                last = mm(PS[:, g * P:(g + 1) * P], hxy[:, g, 1, :], cf("vy"), start=False, stop=True)
            last.then_inc(sem("corners_psum"), 1)
            pe.wait_ge(sem("corners_ready"), 1)
            pe.wait_ge(sem("split_ready"), 4)
            for tp in range(NT // 2):
                if tp >= 2:
                    pe.wait_ge(sem("bound_ready"), tp - 1)
                for tt in range(2):
                    for g in range(G):
                        for j in range(HG):
                            r = slice(32 * j, 32 * j + KROWS)
                            t = 2 * tp + tt
                            at = (4 * (tp % 2) + j) * BANK + (2 * g + tt) * P
                            last = mm(PS[:, at:at + P], QA[g][r, t * P:(t + 1) * P], VV[r, g * P:(g + 1) * P], start=True, stop=True)
                last.then_inc(sem("bound_psum"), 1)
            pe.wait_ge(sem("mr_ready"), 1)
            for g in range(G):
                for t in range(NT):
                    last = mm(PS[:, 4 * g * BANK + t * P:4 * g * BANK + (t + 1) * P], MR[:, g, t, :], cb("identb"), start=True, stop=True)
                last.then_inc(sem("mrows_psum"), 1)
            pe.wait_ge(sem("q_final"), 4)
            pe.sem_inc(sem("q_used"), 1)

            for g in range(G):
                pe.wait_ge(sem("kp_ready"), g + 1)
                with pe.Fori(0, NC) as c:
                    it = c + g * NC

                    def slot_free(fill):
                        prev = fill - 3
                        s = prev // 2
                        if prev % 2 == 0:
                            name, rank, per = copied(s)
                        else:
                            name, rank, per = "l_ready", s + 1, STEPS
                        return name, it * per + rank

                    def pv(n):
                        pe.wait_ge(sem("p_ready"), it * NT + n + 1)
                        for j in range(HG):
                            last = mm(PS[32 * j:32 * j + 32, 6 * BANK:7 * BANK], VS[:, n, g * HG + j, :], PB[n % 2][:, j, :],
                                      start=(n == 0), stop=(n == NT - 1))
                            if n == NT - 2 and j == 0:
                                last.then_inc(sem("q_used"), 1)
                        last.then_inc(sem("pv_done"), 1)

                    pe.wait_ge(sem("q_staged"), it + 1)
                    for n in range(NT):
                        for hp in range(2):
                            s = 2 * n + hp
                            for fill, Q in ((2 * s, QSA), (2 * s + 1, QSB)):
                                if not (fill < 3):
                                    pe.wait_ge(sem(slot_free(fill)[0]), slot_free(fill)[1])
                                elif fill == 0:
                                    pe.wait_ge(sem("sums_taken"), it + 1)
                                for k in range(2):
                                    last = mm(bank(2 * (fill % 3) + k), KP[2 * hp + k][:, n * P:(n + 1) * P], Q[:, :], start=True, stop=True)
                                last.then_inc(sem("scores_done"), 1)
                        if n >= 2:
                            pv(n - 2)
                    pv(NT - 2)
                    pv(NT - 1)

            pe.wait_ge(sem("sums_taken"), G * NC + 1)
            for t in range(NT):
                for g in range(G):
                    last = nc.tensor.transpose(PS[:, (2 * t + g) * P:(2 * t + g + 1) * P], OT[g][:, t * P:(t + 1) * P], ident)
                if t % 4 == 3:
                    last.then_inc(sem("o_psum"), 1)

            def router(l, w, n):
                pe.wait_ge(sem("xt_ready"), NC * (2 * l + 2))
                for t in range(NT):
                    last = mm(PS[:, 4 * BANK + t * n:4 * BANK + (t + 1) * n], XT[:, t * P:(t + 1) * P], w, start=True, stop=True)
                last.then_inc(sem(f"router_psum{l}"), 1)

            def masks_back(l, src, n):
                pe.wait_ge(sem(f"mask_ready{l}"), 1)
                for t in range(NT):
                    last = nc.tensor.transpose(PS[0:n, t * P:(t + 1) * P], src[:, t, 0:n], ident)
                last.then_inc(sem(f"mask_psum{l}"), 1)

            def moe(l):
                m = MOE[l]
                nb, npro = m["n_body"], m["n_pro"]
                gu, down_done, taken = sem(f"gu_done{l}"), sem(f"down_done{l}"), sem(f"su_done{l}")
                for c in range(NC):
                    for t in range(4 * c, 4 * c + 4):
                        mm(PS[:, 4 * BANK + t * P:4 * BANK + (t + 1) * P], X[:, t, :], ident,
                           start=(t == 4 * c), stop=False, skip_group_check=True)

                def down(slot, c, u, buf):
                    o, w = bank(4 + c), slice(2 * P, 3 * P)
                    pe.wait_ge(sem(f"hh_ready{l}"), u + 1)
                    mm(o, WL[:, slot, w], HH[buf][:, :], start=False, stop=False, skip_group_check=True)
                    pe.wait_ge(sem(f"hl_ready{l}"), u + 1)
                    mm(o, WH[:, slot, w], HL[buf][:, :], start=False, stop=False, skip_group_check=True)
                    mm(o, WH[:, slot, w], HH[buf][:, :], start=False, stop=False, skip_group_check=True).then_inc(down_done, 1)

                def run(seq, base, due, it=None, first=False):
                    due = list(due)
                    for k, (slot, c) in enumerate(seq):
                        if it is not None and c == 0:
                            h, i = divmod(slot, m["sub"])
                            pe.wait_ge(sem(f"w_split{l}_{h}"), it * m["sub"] + i + 1)
                        if not (first and k < 2):
                            pe.wait_ge(taken, base + k - 1)
                        x = slice(c * CH, (c + 1) * CH)
                        for i in range(2):
                            o, w = bank(2 * (k % 2) + i), slice(i * P, (i + 1) * P)
                            mm(o, WL[:, slot, w], XH[:, x], start=True, stop=False)
                            mm(o, WH[:, slot, w], XL[:, x], start=False, stop=False)
                            last = mm(o, WH[:, slot, w], XH[:, x], start=False, stop=True)
                        last.then_inc(gu, 1)
                        due.append((slot, c))
                        if len(due) > 3:
                            down(*due.pop(0), base + k - 3, (k + 1) % 4)
                    return due

                pe.wait_ge(sem("x_split"), l + 1)
                if l == 0:
                    pe.wait_ge(sem("wsh_split"), 2)
                    due = run(m["pro"], 0, [], first=True)
                    with pe.Fori(0, m["halves"] // 2) as it:
                        run(m["body"], npro + it * nb, due, it)
                else:
                    due = run(m["body"], 0, [], 0, first=True)
                    with pe.Fori(1, m["halves"] // 2) as it:
                        run(m["body"], it * nb, due, it)
                total = npro + nb * m["halves"] // 2
                for k, unit in ((3, m["body"][-3]), (2, m["body"][-2]), (1, m["body"][-1])):
                    down(*unit, total - k, 4 - k)

            def moe_back(l):
                for q in range(NC):
                    pe.wait_ge(sem("yt_ready"), NC * l + q + 1)
                    for t in range(4 * q, 4 * q + 4):
                        last = nc.tensor.transpose(PS[:, t * P:(t + 1) * P], YT[:, t * P:(t + 1) * P], ident)
                    last.then_inc(sem("y_psum"), 1)

            pe.wait_ge(sem("rest_loaded"), 16 * 8)
            transpose_norm(1)
            router(0, gw0[:, :], E0)
            masks_back(0, sc, E0)
            pe.wait_ge(sem("mask_t0"), 4)
            moe(0)
            moe_back(0)
            transpose_norm(2)

            pe.wait_ge(sem("xt_ready"), NC * 3)
            for t in range(NT):
                last = mm(PS[:, 4 * BANK + t * 64:4 * BANK + (t + 1) * 64], XT[:, t * P:(t + 1) * P], wol[:, :], start=True, stop=True)
            last.then_inc(sem("ol_psum"), 1)
            pe.wait_ge(sem("dx_ready"), 1)
            mm(PS[:, 7 * BANK:7 * BANK + P], cf("ones"), wout[:, :], start=True, stop=True)
            mm(PS[:, 7 * BANK + P:7 * BANK + P + 8], cf("selx"), dx[:, :], start=True, stop=True).then_inc(sem("tables_psum"), 1)
            pe.wait_ge(sem("ts_ready"), 1)
            for t in range(NT):
                last = nc.tensor.transpose(PS[0:96, t * P:(t + 1) * P], TS[:, t, :], ident)
            last.then_inc(sem("ts_psum"), 1)

            pe.wait_ge(sem("tables_ready"), 1)
            pe.wait_ge(sem("ti_ready"), 2)
            fills = [("b", 0), ("b", 1), ("w", 0), ("a", 0), ("r", 0), ("b", 2), ("b", 3), ("w", 1), ("a", 1), ("r", 1)]
            for f, (kind, i) in enumerate(fills):
                base = 4 if f % 2 == 0 else 0
                if f >= 2:
                    k = fills[f - 2][0]
                    n = sum((x == "w") == (k == "w") for x, _ in fills[:f - 1])
                    pe.wait_ge(sem("expanded_act" if k == "w" else "expanded_dve"), n)
                if kind == "r":
                    pe.wait_ge(sem("expanded_dve"), 2 + 4 * i)
                for c in range(NC):
                    x = slice(c * CH, (c + 1) * CH)
                    if kind == "b":
                        last = mm(bank(base + c), cb("selb")[0:32, i * P:(i + 1) * P], TI[0:32, x], start=True, stop=True)
                    elif kind == "a":
                        last = mm(bank(base + c), cb("sela")[32:64, i * P:(i + 1) * P], TI[32:64, x], start=True, stop=True)
                    elif kind == "w":
                        last = mm(bank(base + c), cf("selw")[64:96, i * P:(i + 1) * P], TW[64:96, x], start=True, stop=True)
                    else:
                        mm(bank(base + c), BD[:, 0, :], OH[0][:, x], start=True, stop=False)
                        last = mm(bank(base + c), BD[:, 1, :], OH[1][:, x], start=False, stop=True)
                last.then_inc(sem("expand_psum"), 1)
            pe.wait_ge(sem("expanded_dve"), 8)
            for t in range(NT):
                o = PS[:, 4 * BANK + t * P:4 * BANK + (t + 1) * P]
                mm(o, PR[0][:, t * P:(t + 1) * P], cw[:, :], start=True, stop=False)
                last = mm(o, PR[1][:, t * P:(t + 1) * P], cw[:, :], start=False, stop=True)
                if t % 4 == 3:
                    last.then_inc(sem("lookup_psum"), 1)

            transpose_norm(3)
            router(1, gw1[:, :], E1)
            masks_back(1, sc, E1)
            pe.wait_ge(sem("mask_t1"), 4)
            moe(1)
            moe_back(1)

        @block.scalar
        def _(act):
            A = nc.scalar.activation

            def norm_out(l):
                for q in range(NC):
                    act.wait_ge(sem("xt_psum"), NC * l + q + 1)
                    nc.scalar.copy(XT[:, q * CH:(q + 1) * CH], bank(q)).then_inc(sem("xt_ready"), 1)

            norm_out(0)
            for i in range(6):
                for step in range(2):
                    if step == 0:
                        act.wait_ge(sem("f_ready") if i < 4 else sem("f_scaled"), i + 1 if i < 4 else i - 3)
                        if i >= 3:
                            act.wait_ge(sem("split_ready"), i - 2)
                    else:
                        act.wait_ge(sem("rest1_ready"), i + 1)
                    nc.scalar.copy(TB[i % 3][:, :], F[i][:, :]).then_inc(sem("part_ready"), 1)

            for g in range(G):
                with act.Fori(0, NC) as c:
                    it = c + g * NC

                    def exponential(n):
                        act.wait_ge(sem("l_ready"), it * STEPS + 2 * n + 2)
                        if n >= 2:
                            act.wait_ge(sem("pv_done"), it * NT + n - 1)
                        A(PB[n % 2][:, :, :], LB[n % 2][:, :, :], ACT.Exp).then_inc(sem("p_ready"), 1)

                    for n in range(NT):
                        for s in (2 * n, 2 * n + 1):
                            if s in ACT_COPIES:
                                act.wait_ge(sem("scores_done"), it * FILLS + 2 * s + 1)
                                if s >= 2:
                                    act.wait_ge(sem("l_ready"), it * STEPS + s - 1)
                                sl = 2 * s % 3
                                nc.scalar.copy(ASB[s % 2][:, :], bank(2 * sl, 2)).then_inc(sem("a_copied_act"), 1)
                        if n >= 1:
                            exponential(n - 1)
                    exponential(NT - 1)

            def weights_leading(slot, name):
                nc.scalar.copy(WH[:, slot, :], WR[:, slot, :]).then_inc(sem(name), 1)

            act.wait_ge(sem("o_psum"), NC)
            act.wait_ge(sem("wsh_loaded"), 16)
            for i in range(2):
                weights_leading(2 * SUB0 - 2 + i, "wsh_hi")
            act.wait_ge(sem("w_loaded0_0"), 16)
            for i in range(SUB0):
                weights_leading(i, "w_hi0")

            norm_out(1)
            act.wait_ge(sem("router_psum0"), 1)
            A(sc[:, :, :], bank(4, 2).rearrange("p (t e) -> p t e", e=E0), ACT.Sigmoid).then_inc(sem("scores0_ready"), 1)

            def moe(l):
                m = MOE[l]
                nb, npro = m["n_body"], m["n_pro"]

                def leading(u, buf, first=False):
                    act.wait_ge(sem(f"h_ready{l}"), u + 1)
                    if not first:
                        act.wait_ge(sem(f"down_done{l}"), u - 3)
                    nc.scalar.copy(HH[buf][:, :], HF[buf % 2][:, :]).then_inc(sem(f"hh_ready{l}"), 1)

                def run(seq, base, it=None, first=False):
                    for k in range(len(seq)):
                        act.wait_ge(sem(f"gu_done{l}"), base + k + 1)
                        if not (first and k < 2):
                            act.wait_ge(sem(f"su_done{l}"), base + k - 1)
                        A(SL[k % 2][:, :], bank(2 * (k % 2)), ACT.Silu).then_inc(sem(f"silu_done{l}"), 1)
                        if not (first and k < 1):
                            leading(base + k - 1, (k - 1) % 4, first and k < 5)
                        if it is not None:
                            for half, i, due in splits(m, k):
                                if i == 0:
                                    act.wait_ge(sem(f"w_loaded{l}_{half}"), (it + 2 - half) * 16)
                                    if not (first and due == 0):
                                        act.wait_ge(sem(f"down_done{l}"), base + due)
                                weights_leading(half * m["sub"] + i, f"w_hi{l}")

                if l == 0:
                    run(m["pro"], 0, first=True)
                    with act.Fori(0, m["halves"] // 2) as it:
                        run(m["body"], npro + it * nb, it)
                else:
                    run(m["body"], 0, 0, first=True)
                    with act.Fori(1, m["halves"] // 2) as it:
                        run(m["body"], it * nb, it)
                total = npro + nb * m["halves"] // 2
                leading(total - 1, 3)
                act.wait_ge(sem(f"down_done{l}"), total)
                for q in range(NC):
                    nc.scalar.copy(YT[:, q * CH:(q + 1) * CH], bank(4 + q)).then_inc(sem("yt_ready"), 1)

            moe(0)
            norm_out(2)
            act.wait_ge(sem("logits_ready"), 1)
            A(TS[:, :, 64:96], TS[:, :, 64:96], ACT.Exp).then_inc(sem("exps_ready"), 1)
            act.wait_ge(sem("ts_psum"), 1)
            nc.scalar.copy(TI[:, :], PS[0:64, 0:T]).then_inc(sem("ti_ready"), 1)
            nc.scalar.copy(TW[64:96, :], PS[64:96, 0:T]).then_inc(sem("ti_ready"), 1)
            for m, f in ((0, 3), (1, 8)):
                act.wait_ge(sem("expand_psum"), f)
                if m == 1:
                    act.wait_ge(sem("expanded_dve"), 3)
                nc.scalar.copy(WE[:, :], bank(4 if (f - 1) % 2 == 0 else 0, 4)).then_inc(sem("expanded_act"), 1)

            act.wait_ge(sem("w_loaded1_0"), 16)
            for i in range(SUB1):
                weights_leading(i, "w_hi1")
            norm_out(3)
            act.wait_ge(sem("router1_ready"), 1)
            A(sc[:, :, 0:E1], sc[:, :, 0:E1], ACT.Exp).then_inc(sem("scores1_ready"), 1)
            moe(1)

        @block.gpsimd
        def _(pool):
            gp = nc.gpsimd

            def norm_scale(l):
                pool.wait_ge(sem("moments_ready"), l + 1)
                gp.tensor_scalar(rstd[:, :], moments[:, :, 1], EPS, None, ALU.add).then_inc(sem("var_ready"), 1)
                pool.wait_ge(sem("var_ready"), l + 1)
                gp.tensor_tensor(rstd[:, :], rstd[:, :], half[:, :], ALU.pow).then_inc(sem("rstd_ready"), 1)

            gp.memset(half[:, :], -0.5).then_inc(sem("pool_zero"), 1)
            gp.memset(VS[:, :, :, 16:32], 0.0).then_inc(sem("pool_zero"), 1)
            gp.memset(hxy[:, :, :, :], 0.0).then_inc(sem("pool_zero"), 1)
            gp.memset(MR[:, :, :, :], 0.0).then_inc(sem("pool_zero"), 1)
            pool.wait_ge(sem("pool_zero"), 2)
            gp.memset(VS[:, :, :, 16:17], 1.0).then_inc(sem("pool_zero"), 1)
            norm_scale(0)
            pool.wait_ge(sem("xn_ready"), NC)
            gp.tensor_tensor(XS[:, :, :], X[:, :, :], XN[:, :, :], ALU.add).then_inc(sem("xs_ready"), 1)
            for g in range(G):
                pool.wait_ge(sem("f_ready"), 3 + g)
                gp.tensor_scalar(F[4 + g][:, :], F[2 + g][:, :], 0.2, None, ALU.mult).then_inc(sem("f_scaled"), 1)
            pool.wait_ge(sem("q_final"), 4)
            for g in range(G):
                with pool.Fori(0, NC) as c:
                    it = c + g * NC
                    pool.wait_ge(sem("q_used"), it + 1)
                    gp.tensor_copy(QSA[:, :], QA[g][:, ds(c * CH, CH)])
                    gp.tensor_copy(QSB[:, :], QB[g][:, ds(c * CH, CH)]).then_inc(sem("q_staged"), 1)

            def weights_rest(slot, hi_name, hi_value, done_name):
                pool.wait_ge(sem(hi_name), hi_value)
                gp.tensor_tensor(WL[:, slot, :], WR[:, slot, :], WH[:, slot, :].bitcast(f32), ALU.subtract).then_inc(
                    sem(done_name), 1)

            def split_x(l):
                pool.wait_ge(sem("xt_ready"), NC * (2 * l + 2))
                gp.tensor_copy(XH[:, :], XT[:, :]).then_inc(sem("x_hi"), 1)
                pool.wait_ge(sem("x_hi"), l + 1)
                gp.tensor_tensor(XL[:, :], XT[:, :], XH[:, :].bitcast(f32), ALU.subtract).then_inc(sem("x_split"), 1)

            def split_first(l):
                for i in range(MOE[l]["sub"]):
                    weights_rest(i, f"w_hi{l}", i + 1, f"w_split{l}_0")

            def moe(l):
                m = MOE[l]
                nb, npro, sub = m["n_body"], m["n_pro"], m["sub"]

                def run(seq, base, it=None, first=False):
                    for k, (slot, c) in enumerate(seq):
                        h, s = divmod(slot, sub)
                        if it is not None and c == 0 and s == 0:
                            per = len(SEGMENTS0) if l == 0 else 1
                            pool.wait_ge(sem(f"m_loaded{l}_{h}"), (it + 1) * 16 * per)
                        pool.wait_ge(sem(f"su_done{l}"), base + k + 1)
                        if not (first and k < 2):
                            pool.wait_ge(sem(f"hl_ready{l}"), base + k - 1)
                        if it is None:
                            ins = gp.tensor_copy(HF[k % 2][:, :], SU[k % 2][:, :])
                        else:
                            mask = MK[:, h, s if l == 0 else 0, c * CH:(c + 1) * CH]
                            ins = gp.tensor_tensor(HF[k % 2][:, :], SU[k % 2][:, :], mask, ALU.mult)
                        ins.then_inc(sem(f"h_ready{l}"), 1)
                        if it is not None:
                            for half, i, due in splits(m, k - 1):
                                weights_rest(half * sub + i, f"w_hi{l}", (it * 2 + 2 - half) * sub + i + 1, f"w_split{l}_{half}")

                if l == 0:
                    run(m["pro"], 0, first=True)
                    with pool.Fori(0, m["halves"] // 2) as it:
                        run(m["body"], npro + it * nb, it)
                else:
                    run(m["body"], 0, 0, first=True)
                    with pool.Fori(1, m["halves"] // 2) as it:
                        run(m["body"], it * nb, it)

            norm_scale(1)
            for i in range(2):
                weights_rest(2 * SUB0 - 2 + i, "wsh_hi", i + 1, "wsh_split")
            split_x(0)
            split_first(0)
            moe(0)
            norm_scale(2)
            pool.wait_ge(sem("x_moe0"), NC)
            gp.tensor_tensor(XS[:, :, :], X[:, :, :], boutb[:, :].unsqueeze(1).to_broadcast([P, NT, P]),
                             ALU.add).then_inc(sem("xs_ready"), 1)
            split_first(1)
            norm_scale(3)
            split_x(1)
            moe(1)

        @block.vector
        def _(dve):
            v = nc.vector
            TS_, TT, STT = v.tensor_scalar, v.tensor_tensor, v.scalar_tensor_tensor

            def after(ins, name, n):
                ins.then_inc(sem(name), 1)
                dve.wait_ge(sem(name), n)

            def norm(l):
                for t in range(NT):
                    last = v.bn_stats(stats[:, t, :], X[:, t, :])
                after(last, "stats_ready", l + 1)
                for t in range(NT):
                    last = v.bn_aggr(moments[:, t, :], stats[:, t, :])
                after(last, "moments_ready", l + 1)
                dve.wait_ge(sem("rstd_ready"), l + 1)
                for t in range(NT):
                    last = TS_(XN[:, t, :], X[:, t, :], moments[:, t, 0:1], rstd[:, t:t + 1], ALU.subtract, ALU.mult)
                    if t % 4 == 3:
                        last.then_inc(sem("xn_ready"), 1)

            dve.wait_ge(sem("x_loaded"), 16)
            norm(0)
            dve.wait_ge(sem("cb_loaded"), 16)
            dve.wait_ge(sem("cf_loaded"), 16)
            v.tensor_copy(CB[:, :], YT[:, 0:NB]).then_inc(sem("cb_ready"), 1)

            dve.wait_ge(sem("qkv_loaded"), 64)
            for i in range(4):
                dve.wait_ge(sem("proj_done"), i + 1)
                TS_(F[i][:, :], bank(4 * ((i + 1) % 2), 4), bqk[:, i:i + 1], 1.0 if i < 2 else 1 / math.sqrt(DQK),
                    ALU.add, ALU.mult).then_inc(sem("f_ready"), 1)
            dve.wait_ge(sem("v_psum"), 1)
            dve.wait_ge(sem("pool_zero"), 5)
            TT(VS[:, :, :, 0:DV], bank(4, 4).rearrange("p (t h d) -> p t h d", h=H, d=DV),
               bvb[:, :].rearrange("p (h d) -> p h d", d=DV).unsqueeze(1).to_broadcast([P, NT, H, DV]),
               ALU.add).then_inc(sem("v_ready"), 1)
            targets = [KS[0], KS[1], QA[0], QA[1], QB[0], QB[1]]

            def split(i):
                sel = cf("ksel") if i < 2 else cf("qsel")
                if i in (2, 3):
                    dve.wait_ge(sem("f_scaled"), i - 1)
                dve.wait_ge(sem("part_ready"), 2 * i + 1)
                STT(F[i][:, :], TB[i % 3][:, :], sel[:, 0:1], F[i][:, :], ALU.mult, ALU.add).then_inc(sem("rest1_ready"), 1)
                dve.wait_ge(sem("part_ready"), 2 * i + 2)
                STT(targets[i][:, :], TB[i % 3][:, :], sel[:, 1:2], F[i][:, :], ALU.mult, ALU.add).then_inc(sem("split_ready"), 1)

            split(0)
            split(1)
            split(2)
            split(3)
            for h in range(H):
                dve.wait_ge(sem("extent_psum"), h + 1)
                last = v.reduce_max(hm[:, h:h + 1], bank(4 * (h % 2), 4), AX.X)
                last.then_inc(sem("extent_ready"), 1)
            dve.wait_ge(sem("extent_ready"), H)
            for d in range(DQK):
                last = v.tensor_copy(hxy[:, :, d, :].rearrange("p g (j r) -> p g j r", r=32)[:, :, :, 9 * d:9 * d + 9],
                                     hm[:, :].rearrange("p (g j) -> p g j", g=G).unsqueeze(3).to_broadcast([P, G, HG, 9]))
            last.then_inc(sem("hxy_ready"), 1)
            dve.wait_ge(sem("corners_psum"), 1)
            after(v.tensor_copy(vtx[:, :], PS[:, 0:G * P]), "corner_step", 1)
            after(v.tensor_copy(vtb[:, :], vtx[:, :]), "corner_step", 2)
            after(STT(vtx[:, :], vtb[:, :], cf("ksel")[:, 0:1], vtx[:, :], ALU.mult, ALU.add), "corner_step", 3)
            after(v.tensor_copy(vtb[:, :], vtx[:, :]), "corner_step", 4)
            STT(VV[:, :], vtb[:, :], cf("ksel")[:, 1:2], vtx[:, :], ALU.mult, ALU.add).then_inc(sem("corners_ready"), 1)
            split(4)
            split(5)
            bound, neg, rest, tmp = (small[:, i, :] for i in range(4))
            for tp in range(NT // 2):
                dve.wait_ge(sem("bound_psum"), tp + 1)
                v.reduce_max(bound[:, tp * 16:(tp + 1) * 16],
                             bank(4 * (tp % 2), 4).rearrange("p (a b) -> p a b", b=P), AX.X).then_inc(sem("bound_ready"), 1)
            dve.wait_ge(sem("bound_ready"), NT // 2)
            after(STT(tmp, bound, 0.2, bound, ALU.mult, ALU.max), "max_step", 1)
            after(TS_(neg, tmp, -1.0, None, ALU.mult), "max_step", 2)
            after(v.tensor_copy(mparts[:, 0, :], neg), "max_step", 3)
            after(TT(rest, neg, mparts[:, 0, :], ALU.subtract), "max_step", 4)
            after(v.tensor_copy(mparts[:, 1, :], rest), "max_step", 5)
            after(TT(mparts[:, 2, :], rest, mparts[:, 1, :], ALU.subtract), "max_step", 6)
            mv = mparts[:, :, :].rearrange("p k (tp j g tt) -> p g tt tp j k", j=HG, g=G, tt=2)
            for g in range(G):
                o = MR[:, g, :, :].rearrange("p (tp tt) (j r) -> p tt tp j r", tt=2, r=32)
                for tt in range(2):
                    last = v.tensor_copy(o[:, tt, :, :, KROWS:KSC], mv[:, g, tt])
            last.then_inc(sem("mr_ready"), 1)
            for g in range(G):
                dve.wait_ge(sem("mrows_psum"), g + 1)
                for Q in (QA[g], QB[g]):
                    TT(Q[:, :], bank(4 * g, 4), Q[:, :], ALU.add).then_inc(sem("q_final"), 1)
            dve.sem_inc(sem("sums_taken"), 1)

            for g in range(G):
                for j in range(HG):
                    last = TS_(KP[j][:, :], KS[g][:, :], cf("hmask")[:, j:j + 1], None, ALU.mult)
                last.then_inc(sem("kp_ready"), 1)
                with dve.Fori(0, NC) as c:
                    it = c + g * NC
                    for s in range(STEPS):
                        n, hp = divmod(s, 2)
                        if s in DVE_COPIES:
                            dve.wait_ge(sem("scores_done"), it * FILLS + 2 * s + 1)
                            v.tensor_copy(ASB[s % 2][:, :], bank(2 * (2 * s % 3), 2)).then_inc(sem("a_copied_dve"), 1)
                        name, rank, per = copied(s)
                        dve.wait_ge(sem(name), it * per + rank)
                        dve.wait_ge(sem("scores_done"), it * FILLS + 2 * s + 2)
                        if n >= 2 and hp == 0:
                            dve.wait_ge(sem("p_ready"), it * NT + n - 1)
                        TT(LB[n % 2][:, 2 * hp:2 * hp + 2, :],
                           bank(2 * ((2 * s + 1) % 3), 2).rearrange("p (j q) -> p j q", j=2),
                           ASB[s % 2][:, :].rearrange("p (j q) -> p j q", j=2), ALU.max).then_inc(sem("l_ready"), 1)
                    dve.wait_ge(sem("pv_done"), (it + 1) * NT)
                    v.tensor_copy(OT[g][:, ds(c * CH, CH)], bank(6)).then_inc(sem("sums_taken"), 1)

            dve.wait_ge(sem("rest_loaded"), 16 * 8)
            dve.wait_ge(sem("xs_ready"), 1)
            og = small[:, 0, :]
            for q in range(NC):
                dve.wait_ge(sem("o_psum"), q + 1)
                o = bank(2 * q, 2).rearrange("p (a b) -> p a b", b=32)
                ogq = og[:, q * 32:(q + 1) * 32]
                tq = YT[:, q * CH:(q + 1) * CH].rearrange("p (a b) -> p a b", b=DV)
                after(v.reciprocal(ogq, o[:, :, DV]), "o_step", 4 * q + 1)
                after(TS_(ogq, ogq, gam[:, 0:1], None, ALU.mult), "o_step", 4 * q + 2)
                after(TT(tq, o[:, :, 0:DV], ogq.unsqueeze(2).to_broadcast([P, 32, DV]), ALU.mult), "o_step", 4 * q + 3)
                after(TT(X[:, 4 * q:4 * q + 4, :], XS[:, 4 * q:4 * q + 4, :],
                         YT[:, q * CH:(q + 1) * CH].rearrange("p (t c) -> p t c", c=P), ALU.add), "o_step", 4 * q + 4)

            norm(1)

            def masks_out(l, n):
                dve.wait_ge(sem(f"mask_psum{l}"), 1)
                for q in range(NC):
                    v.tensor_copy(MT[0:n, q * CH:(q + 1) * CH], PS[0:n, q * BANK:(q + 1) * BANK]).then_inc(sem(f"mask_t{l}"), 1)

            def choose(l, n, k, scores, key):
                for t in range(NT):
                    last = v.max(top8[:, t, :], key[:, t, 0:n])
                after(last, f"top_step{l}", 1)
                after(v.memset(top8[:, :, k:8], -3e38), f"top_step{l}", 2)
                for t in range(NT):
                    last = v.match_replace(rp[:, t, 0:n], top8[:, t, :], key[:, t, 0:n], -1e30)
                after(last, f"top_step{l}", 3)
                after(TT(rp[:, :, 0:n], rp[:, :, 0:n], key[:, :, 0:n], ALU.not_equal), f"top_step{l}", 4)
                after(TT(scores[:, :, 0:n], scores[:, :, 0:n], rp[:, :, 0:n], ALU.mult), f"top_step{l}", 5)
                after(v.reduce_sum(rsum[:, :], scores[:, :, 0:n], AX.X), f"top_step{l}", 6)

            dve.wait_ge(sem("scores0_ready"), 1)
            after(TT(bs[:, :, :], sc[:, :, :], gb0[:, :].unsqueeze(1).to_broadcast([P, NT, E0]), ALU.add), "keys_ready", 1)
            choose(0, E0, TOP0, sc, bs)
            after(TS_(rsum[:, :], rsum[:, :], 1e-20, None, ALU.add), "top_step0", 7)
            after(v.reciprocal(rsum[:, :], rsum[:, :]), "top_step0", 8)
            after(TT(sc[:, :, :], sc[:, :, :], rsum[:, :].unsqueeze(2).to_broadcast([P, NT, E0]), ALU.mult), "top_step0", 9)
            TS_(sc[:, :, :], sc[:, :, :], SCALE0, None, ALU.mult).then_inc(sem("mask_ready0"), 1)
            masks_out(0, E0)

            def moe(l):
                m = MOE[l]
                nb, npro = m["n_body"], m["n_pro"]

                def rest_of(u, buf, first=False):
                    dve.wait_ge(sem(f"hh_ready{l}"), u + 1)
                    if not first:
                        dve.wait_ge(sem(f"down_done{l}"), u - 3)
                    TT(HL[buf][:, :], HF[buf % 2][:, :], HH[buf][:, :].bitcast(f32), ALU.subtract).then_inc(sem(f"hl_ready{l}"), 1)

                def run(seq, base, first=False):
                    for k in range(len(seq)):
                        dve.wait_ge(sem(f"silu_done{l}"), base + k + 1)
                        if not (first and k < 2):
                            dve.wait_ge(sem(f"h_ready{l}"), base + k - 1)
                        TT(SU[k % 2][:, :], bank(2 * (k % 2) + 1), SL[k % 2][:, :], ALU.mult).then_inc(sem(f"su_done{l}"), 1)
                        if not (first and k < 1):
                            rest_of(base + k - 1, (k - 1) % 4, first and k < 5)

                if l == 0:
                    run(m["pro"], 0, first=True)
                    with dve.Fori(0, m["halves"] // 2) as it:
                        run(m["body"], npro + it * nb)
                else:
                    run(m["body"], 0, first=True)
                    with dve.Fori(1, m["halves"] // 2) as it:
                        run(m["body"], it * nb)
                rest_of(npro + nb * m["halves"] // 2 - 1, 3)
                for q in range(NC):
                    dve.wait_ge(sem("y_psum"), NC * l + q + 1)
                    last = v.tensor_copy(X[:, 4 * q:4 * q + 4, :], bank(q).rearrange("p (t c) -> p t c", c=P))
                    last.then_inc(sem(f"x_moe{l}"), 1)
                dve.wait_ge(sem(f"x_moe{l}"), NC)

            moe(0)
            norm(2)

            dve.wait_ge(sem("xt_ready"), 2 * NC + 1)
            TS_(dx[:, :], cf("amask"), XT[:, 0:1], None, ALU.mult).then_inc(sem("dx_ready"), 1)
            dve.wait_ge(sem("ol_psum"), 1)
            after(TT(OL[:, :, :], bank(4, 2).rearrange("p (t e) -> p t e", e=2 * HP),
                     bol[:, :].unsqueeze(1).to_broadcast([P, NT, 2 * HP]), ALU.add), "ol_ready", 1)
            lg = OL[:, :, HP:2 * HP].rearrange("p t (h k) -> p t h k", k=PT)
            wt = TS[:, :, 64:96].rearrange("p t (h k) -> p t h k", k=PT)
            after(v.reduce_max(lmax[:, :, :], lg, AX.X), "lk_step", 1)
            TT(wt, lg, lmax[:, :, :].unsqueeze(3).to_broadcast([P, NT, 8, PT]), ALU.subtract).then_inc(sem("logits_ready"), 1)
            off = OL[:, :, 0:HP]
            mag, frac, ng, idx = (i[:, :, :] for i in ix)
            after(STT(mag, off, -1.0, off, ALU.mult, ALU.max), "lk_step", 2)
            after(TS_(mag, mag, 300.0, None, ALU.min), "lk_step", 3)
            TS_(ng, off, -1.0, None, ALU.is_le)
            after(v.tensor_copy(iint[:, :, :], mag), "lk_step", 4)
            after(v.tensor_copy(frac, iint[:, :, :]), "lk_step", 5)
            after(TT(idx, frac, mag, ALU.is_gt), "lk_step", 6)
            after(TT(mag, frac, idx, ALU.subtract), "lk_step", 7)
            after(TS_(frac, mag, -2.0, float(P), ALU.mult, ALU.add), "lk_step", 8)
            after(TT(frac, frac, ng, ALU.mult), "lk_step", 9)
            after(TT(idx, mag, frac, ALU.add), "lk_step", 10)
            after(TS_(idx, idx, 0.0, P - 1.0, ALU.max, ALU.min), "lk_step", 11)
            hi = TS[:, :, 32:64]
            after(TS_(mag, idx, 1 / 16, None, ALU.mult), "lk_step", 12)
            after(v.tensor_copy(iint[:, :, :], mag), "lk_step", 13)
            after(v.tensor_copy(frac, iint[:, :, :]), "lk_step", 14)
            after(TT(ng, frac, mag, ALU.is_gt), "lk_step", 15)
            after(TT(hi, frac, ng, ALU.subtract), "lk_step", 16)
            after(TS_(mag, hi, -16.0, None, ALU.mult), "lk_step", 17)
            TT(TS[:, :, 0:32], mag, idx, ALU.add)
            dve.wait_ge(sem("exps_ready"), 1)
            after(v.reduce_sum(lmax[:, :, :], wt, AX.X), "lk_step", 18)
            after(v.reciprocal(lmax[:, :, :], lmax[:, :, :]), "lk_step", 19)
            TT(wt, wt, lmax[:, :, :].unsqueeze(3).to_broadcast([P, NT, 8, PT]), ALU.mult).then_inc(sem("ts_ready"), 1)
            dve.wait_ge(sem("tables_psum"), 1)
            v.tensor_copy(cw[:, :], PS[:, 7 * BANK:7 * BANK + P])
            after(v.memset(BD[:, :, :], 0.0), "lk_step", 20)
            for k in range(2):
                last = TT(BD[:, k, 64 * k:64 * k + 64].rearrange("p (h q) -> p h q", q=8),
                          PS[:, 7 * BANK + P:7 * BANK + P + 8].unsqueeze(1).to_broadcast([P, 8, 8]),
                          cf("bdmask").rearrange("p (h q) -> p h q", q=8), ALU.mult)
            last.then_inc(sem("tables_ready"), 1)
            for m in range(2):
                for k in range(2):
                    f = 5 * m + k
                    dve.wait_ge(sem("expand_psum"), f + 1)
                    TS_(OH[k][:, :], bank(4 if f % 2 == 0 else 0, 4), cf("bval"), None, ALU.is_equal).then_inc(sem("expanded_dve"), 1)
                f = 5 * m + 3
                dve.wait_ge(sem("expand_psum"), f + 1)
                dve.wait_ge(sem("expanded_act"), m + 1)
                STT(AW[:, :], bank(4 if f % 2 == 0 else 0, 4), cf("aval"), WE[:, :], ALU.is_equal, ALU.mult).then_inc(
                    sem("expanded_dve"), 1)
                f += 1
                dve.wait_ge(sem("expand_psum"), f + 1)
                dve.wait_ge(sem("expanded_dve"), 4 * m + 3)
                TT(PR[m][:, :], bank(4 if f % 2 == 0 else 0, 4), AW[:, :], ALU.mult).then_inc(sem("expanded_dve"), 1)
            dve.wait_ge(sem("xs_ready"), 2)
            for q in range(NC):
                dve.wait_ge(sem("lookup_psum"), q + 1)
                last = TT(X[:, 4 * q:4 * q + 4, :], XS[:, 4 * q:4 * q + 4, :],
                          bank(4 + q).rearrange("p (t c) -> p t c", c=P), ALU.add)
            after(last, "x_lookup", 1)

            norm(3)
            dve.wait_ge(sem("router_psum1"), 1)
            lg = PS[:, 4 * BANK:4 * BANK + NT * E1].rearrange("p (t e) -> p t e", e=E1)
            after(v.reduce_max(rsum[:, :], lg, AX.X), "r1_step", 1)
            TT(sc[:, :, 0:E1], lg, rsum[:, :].unsqueeze(2).to_broadcast([P, NT, E1]), ALU.subtract).then_inc(sem("router1_ready"), 1)
            dve.wait_ge(sem("scores1_ready"), 1)
            after(v.reduce_sum(rsum[:, :], sc[:, :, 0:E1], AX.X), "r1_step", 2)
            after(v.reciprocal(rsum[:, :], rsum[:, :]), "r1_step", 3)
            after(TT(sc[:, :, 0:E1], sc[:, :, 0:E1], rsum[:, :].unsqueeze(2).to_broadcast([P, NT, E1]), ALU.mult), "r1_step", 4)
            after(v.tensor_copy(bs[:, :, 0:E1], sc[:, :, 0:E1]), "r1_step", 5)
            choose(1, E1, TOP1, sc, bs)
            after(v.reciprocal(rsum[:, :], rsum[:, :]), "r1_step", 6)
            TT(sc[:, :, 0:E1], sc[:, :, 0:E1], rsum[:, :].unsqueeze(2).to_broadcast([P, NT, E1]), ALU.mult).then_inc(sem("mask_ready1"), 1)
            masks_out(1, E1)
            moe(1)


_OUT_SHAPE = (1, T, P)


def _layout(i):
    f = {k: np.asarray(v) for k, v in i.items()}
    d = {"x": f["L0_attn_x"].reshape(T, P), "consts": constants()}
    wqk, bqk = np.zeros((P, 4, P), np.float32), np.zeros((P, 4), np.float32)
    for n, w, b in ((0, f["L0_attn_Wk"], f["L0_attn_bk"]), (2, f["L0_attn_Wq"], f["L0_attn_bq"])):
        for h in range(H):
            g, j = divmod(h, HG)
            for r in range(KROWS):
                wqk[:, n + g, 32 * j + r] = w[DQK * h + r // 9]
                bqk[32 * j + r, n + g] = b[DQK * h + r // 9]
            if n == 0:
                bqk[32 * j + KROWS:32 * j + KSC, g] = 1.0
    d["wqk"], d["bqk"] = wqk, bqk
    d["wvt"] = f["L0_attn_Wv"].T
    d["bv"], d["gamma"] = f["L0_attn_bv"], f["L0_attn_gamma"]
    d["gw0"], d["gb0"] = f["L0_ffn_gate_w"], f["L0_ffn_gate_bias"]

    def weights(gate, up, down, halves):
        parts = [gate.reshape(P, halves, -1, P), up.reshape(P, halves, -1, P),
                 down.reshape(halves, -1, P, P).transpose(2, 0, 1, 3)]
        return np.concatenate(parts, 3).transpose(1, 0, 2, 3)

    g0 = f["L0_ffn_all_gate_proj"].transpose(1, 0, 2).reshape(P, -1)
    u0 = f["L0_ffn_all_up_proj"].transpose(1, 0, 2).reshape(P, -1)
    d["w0"] = weights(g0, u0, f["L0_ffn_all_down_proj"].reshape(-1, P), HALVES0)
    pad = 2 * P - f["L0_ffn_sh_gate"].shape[1]
    d["wsh"] = weights(np.pad(f["L0_ffn_sh_gate"], ((0, 0), (0, pad))), np.pad(f["L0_ffn_sh_up"], ((0, 0), (0, pad))),
                       np.pad(f["L0_ffn_sh_down"], ((0, pad), (0, 0))), 1)[0]
    d["wol"] = np.concatenate([f["L1_attn_W_off"][:, 0::2], f["L1_attn_W_attn"]], 1)
    d["bol"] = np.concatenate([f["L1_attn_b_off"][0::2], f["L1_attn_b_attn"]])
    d["wout"], d["bout"] = f["L1_attn_W_out"], f["L1_attn_b_out"]
    d["gw1"] = f["L1_ffn_gate_w"].T
    gu = f["L1_ffn_gate_up_proj"].reshape(E1, 2, -1, P)
    d["w1"] = weights(gu[:, 0].transpose(2, 0, 1).reshape(P, -1), gu[:, 1].transpose(2, 0, 1).reshape(P, -1),
                      f["L1_ffn_down_proj"].transpose(0, 2, 1).reshape(-1, P), HALVES1)
    return {k: np.ascontiguousarray(v, np.float32) for k, v in d.items()}


def kernel(**inputs):
    import concourse.bacc as bacc
    from concourse.bass_utils import run_bass_kernel_spmd as run

    nc = bacc.Bacc("TRN2", target_bir_lowering=False, num_devices=1)
    arrays, args = {}, {}
    for name, v in _layout(inputs).items():
        arrays[f"in_{name}"] = v
        args[name] = nc.dram_tensor(f"in_{name}", v.shape, mybir.dt.float32, kind="ExternalInput").ap()
    out = nc.dram_tensor("out_0", (T, P), mybir.dt.float32, kind="ExternalOutput").ap()
    build(nc, args, out)
    r = run(nc, [arrays], core_ids=[0])
    return r.results[0]["out_0"].reshape(_OUT_SHAPE)
```
